# Optimizing a Trainium2 kernel written in Bass

```python
import numpy as np
import jax
import jax.numpy as jnp

def _softmax(x, axis=-1):
    return jax.nn.softmax(x, axis=axis)

def _gelu(x):
    return jax.nn.gelu(x, approximate=True)

def _silu(x):
    return jax.nn.silu(x)

def _sigmoid(x):
    return jax.nn.sigmoid(x)

def _layernorm(x, axis=-1, eps=1e-05):
    m = jnp.mean(x, axis=axis, keepdims=True)
    v = jnp.var(x, axis=axis, keepdims=True)
    return (x - m) / jnp.sqrt(v + eps)

def _scatter_add(tgt, idx, src, axis=0):
    return tgt.at[idx].add(src)

def _segment_sum(src, seg, n):
    return jax.ops.segment_sum(src, seg, n)
kernel_name = 'mk_dlrm_tower_d1_rec_r8_939ece'

def setup_inputs(seed: int=0):
    np.random.seed(seed)
    _w = jnp.asarray

    def _rec_inputs():
        import jax
        import jax.numpy as jnp
        _tk = jax.random.key(seed)
        dense_ctx = jax.random.normal(jax.random.fold_in(_tk, 190), (512, 16), jnp.float32)
        ids = jnp.stack([jax.random.randint(jax.random.fold_in(_tk, 200 + f), (512,), 0, v, jnp.int32) for f, v in enumerate([1000, 125000, 12500, 125000, 1250, 125000, 12500, 1250, 125000, 1000, 125000, 12500, 1000, 125000, 1250, 1000, 125000, 12500, 1000, 12500, 1000, 1000, 1250, 1000, 1000, 1000])], axis=1)
        tbl_0 = 0.05 * jax.random.normal(jax.random.fold_in(_tk, 500 + 0), (1000, 32), jnp.float32)
        tbl_1 = 0.05 * jax.random.normal(jax.random.fold_in(_tk, 500 + 1), (125000, 32), jnp.float32)
        tbl_2 = 0.05 * jax.random.normal(jax.random.fold_in(_tk, 500 + 2), (12500, 32), jnp.float32)
        tbl_3 = 0.05 * jax.random.normal(jax.random.fold_in(_tk, 500 + 3), (125000, 32), jnp.float32)
        tbl_4 = 0.05 * jax.random.normal(jax.random.fold_in(_tk, 500 + 4), (1250, 32), jnp.float32)
        tbl_5 = 0.05 * jax.random.normal(jax.random.fold_in(_tk, 500 + 5), (125000, 32), jnp.float32)
        tbl_6 = 0.05 * jax.random.normal(jax.random.fold_in(_tk, 500 + 6), (12500, 32), jnp.float32)
        tbl_7 = 0.05 * jax.random.normal(jax.random.fold_in(_tk, 500 + 7), (1250, 32), jnp.float32)
        tbl_8 = 0.05 * jax.random.normal(jax.random.fold_in(_tk, 500 + 8), (125000, 32), jnp.float32)
        tbl_9 = 0.05 * jax.random.normal(jax.random.fold_in(_tk, 500 + 9), (1000, 32), jnp.float32)
        tbl_10 = 0.05 * jax.random.normal(jax.random.fold_in(_tk, 500 + 10), (125000, 32), jnp.float32)
        tbl_11 = 0.05 * jax.random.normal(jax.random.fold_in(_tk, 500 + 11), (12500, 32), jnp.float32)
        tbl_12 = 0.05 * jax.random.normal(jax.random.fold_in(_tk, 500 + 12), (1000, 32), jnp.float32)
        tbl_13 = 0.05 * jax.random.normal(jax.random.fold_in(_tk, 500 + 13), (125000, 32), jnp.float32)
        tbl_14 = 0.05 * jax.random.normal(jax.random.fold_in(_tk, 500 + 14), (1250, 32), jnp.float32)
        tbl_15 = 0.05 * jax.random.normal(jax.random.fold_in(_tk, 500 + 15), (1000, 32), jnp.float32)
        tbl_16 = 0.05 * jax.random.normal(jax.random.fold_in(_tk, 500 + 16), (125000, 32), jnp.float32)
        tbl_17 = 0.05 * jax.random.normal(jax.random.fold_in(_tk, 500 + 17), (12500, 32), jnp.float32)
        tbl_18 = 0.05 * jax.random.normal(jax.random.fold_in(_tk, 500 + 18), (1000, 32), jnp.float32)
        tbl_19 = 0.05 * jax.random.normal(jax.random.fold_in(_tk, 500 + 19), (12500, 32), jnp.float32)
        tbl_20 = 0.05 * jax.random.normal(jax.random.fold_in(_tk, 500 + 20), (1000, 32), jnp.float32)
        tbl_21 = 0.05 * jax.random.normal(jax.random.fold_in(_tk, 500 + 21), (1000, 32), jnp.float32)
        tbl_22 = 0.05 * jax.random.normal(jax.random.fold_in(_tk, 500 + 22), (1250, 32), jnp.float32)
        tbl_23 = 0.05 * jax.random.normal(jax.random.fold_in(_tk, 500 + 23), (1000, 32), jnp.float32)
        tbl_24 = 0.05 * jax.random.normal(jax.random.fold_in(_tk, 500 + 24), (1000, 32), jnp.float32)
        tbl_25 = 0.05 * jax.random.normal(jax.random.fold_in(_tk, 500 + 25), (1000, 32), jnp.float32)
        _rk = jax.random.fold_in(_tk, 7)
        W_top1 = 0.0606339 * jax.random.normal(jax.random.fold_in(_tk, 801), (272, 512), jnp.float32)
        W_top2 = 0.0441942 * jax.random.normal(jax.random.fold_in(_tk, 802), (512, 256), jnp.float32)
        W_top3 = 0.0625 * jax.random.normal(jax.random.fold_in(_tk, 803), (256, 1), jnp.float32)
        b_top1 = jnp.zeros((512,), jnp.float32)
        b_top2 = jnp.zeros((256,), jnp.float32)
        return (dense_ctx, ids, tbl_0, tbl_1, tbl_2, tbl_3, tbl_4, tbl_5, tbl_6, tbl_7, tbl_8, tbl_9, tbl_10, tbl_11, tbl_12, tbl_13, tbl_14, tbl_15, tbl_16, tbl_17, tbl_18, tbl_19, tbl_20, tbl_21, tbl_22, tbl_23, tbl_24, tbl_25, W_top1, b_top1, W_top2, b_top2, W_top3)
    dense_ctx, ids, tbl_0, tbl_1, tbl_2, tbl_3, tbl_4, tbl_5, tbl_6, tbl_7, tbl_8, tbl_9, tbl_10, tbl_11, tbl_12, tbl_13, tbl_14, tbl_15, tbl_16, tbl_17, tbl_18, tbl_19, tbl_20, tbl_21, tbl_22, tbl_23, tbl_24, tbl_25, W_top1, b_top1, W_top2, b_top2, W_top3 = _rec_inputs()

    def _L0_rec_setup():
        import jax, jax.numpy as jnp
        import numpy as np
        M_FIELDS = 26
        H1 = 128
        H2 = 128
        BATCH = 256
        EMB_K = 32

        def _cin_layer(x_prev, x0, W, b):
            return jnp.einsum('bik,bjk,hij->bhk', x_prev, x0, W) + b[None, :, None]
        key = jax.random.key(seed)
        k0, k1, k2, k3, k4 = jax.random.split(key, 5)
        inputs = jax.random.normal(k0, (BATCH, M_FIELDS, EMB_K), dtype=jnp.float32)
        W1 = jax.random.normal(k1, (H1, M_FIELDS, M_FIELDS), dtype=jnp.float32) * 0.05
        b1 = jax.random.normal(k2, (H1,), dtype=jnp.float32) * 0.05
        W2 = jax.random.normal(k3, (H2, H1, M_FIELDS), dtype=jnp.float32) * 0.05
        b2 = jax.random.normal(k4, (H2,), dtype=jnp.float32) * 0.05
        return {'inputs': inputs, 'W1': W1, 'b1': b1, 'W2': W2, 'b2': b2}
    _L0_rec_all = _L0_rec_setup()
    _L0_rec_in = {k: v for k, v in _L0_rec_all.items() if k in ('W1', 'b1', 'W2', 'b2')}
    del _L0_rec_all
    return {'dense_ctx': dense_ctx, 'ids': ids, 'tbl_0': tbl_0, 'tbl_1': tbl_1, 'tbl_2': tbl_2, 'tbl_3': tbl_3, 'tbl_4': tbl_4, 'tbl_5': tbl_5, 'tbl_6': tbl_6, 'tbl_7': tbl_7, 'tbl_8': tbl_8, 'tbl_9': tbl_9, 'tbl_10': tbl_10, 'tbl_11': tbl_11, 'tbl_12': tbl_12, 'tbl_13': tbl_13, 'tbl_14': tbl_14, 'tbl_15': tbl_15, 'tbl_16': tbl_16, 'tbl_17': tbl_17, 'tbl_18': tbl_18, 'tbl_19': tbl_19, 'tbl_20': tbl_20, 'tbl_21': tbl_21, 'tbl_22': tbl_22, 'tbl_23': tbl_23, 'tbl_24': tbl_24, 'tbl_25': tbl_25, 'W_top1': W_top1, 'b_top1': b_top1, 'W_top2': W_top2, 'b_top2': b_top2, 'W_top3': W_top3, 'L0_rec_W1': _L0_rec_in['W1'], 'L0_rec_b1': _L0_rec_in['b1'], 'L0_rec_W2': _L0_rec_in['W2'], 'L0_rec_b2': _L0_rec_in['b2']}

def reference(dense_ctx, ids, tbl_0, tbl_1, tbl_2, tbl_3, tbl_4, tbl_5, tbl_6, tbl_7, tbl_8, tbl_9, tbl_10, tbl_11, tbl_12, tbl_13, tbl_14, tbl_15, tbl_16, tbl_17, tbl_18, tbl_19, tbl_20, tbl_21, tbl_22, tbl_23, tbl_24, tbl_25, W_top1, b_top1, W_top2, b_top2, W_top3, L0_rec_W1, L0_rec_b1, L0_rec_W2, L0_rec_b2):
    import jax
    import jax.numpy as jnp

    def _L0_rec_ref(inputs, W1, b1, W2, b2):
        import jax, jax.numpy as jnp
        import numpy as np
        M_FIELDS = 26
        H1 = 128
        H2 = 128
        BATCH = 256
        EMB_K = 32

        def _cin_layer(x_prev, x0, W, b):
            return jnp.einsum('bik,bjk,hij->bhk', x_prev, x0, W) + b[None, :, None]
        x1 = _cin_layer(inputs, inputs, W1, b1)
        x2 = _cin_layer(x1, inputs, W2, b2)
        res = jnp.concatenate([x1, x2], axis=1)
        return jnp.sum(res, axis=-1)
    e = jnp.stack([tbl_0[ids[:, 0]], tbl_1[ids[:, 1]], tbl_2[ids[:, 2]], tbl_3[ids[:, 3]], tbl_4[ids[:, 4]], tbl_5[ids[:, 5]], tbl_6[ids[:, 6]], tbl_7[ids[:, 7]], tbl_8[ids[:, 8]], tbl_9[ids[:, 9]], tbl_10[ids[:, 10]], tbl_11[ids[:, 11]], tbl_12[ids[:, 12]], tbl_13[ids[:, 13]], tbl_14[ids[:, 14]], tbl_15[ids[:, 15]], tbl_16[ids[:, 16]], tbl_17[ids[:, 17]], tbl_18[ids[:, 18]], tbl_19[ids[:, 19]], tbl_20[ids[:, 20]], tbl_21[ids[:, 21]], tbl_22[ids[:, 22]], tbl_23[ids[:, 23]], tbl_24[ids[:, 24]], tbl_25[ids[:, 25]]], axis=1)
    z = _L0_rec_ref(e, L0_rec_W1, L0_rec_b1, L0_rec_W2, L0_rec_b2)
    z = z.reshape(z.shape[0], -1)
    h = jnp.concatenate([z, dense_ctx], axis=1)
    h = jnp.maximum(h @ W_top1 + b_top1, 0.0)
    h = jnp.maximum(h @ W_top2 + b_top2, 0.0)
    y = h @ W_top3
    return y

_drawn_inputs = setup_inputs


def setup_inputs(seed=0):
    import zlib

    import numpy as np

    out = dict(_drawn_inputs(seed))
    spreads = {'b_top1': (0.0, 0.8), 'b_top2': (0.0, 0.8)}
    factors = {'tbl_0': 8.0,
     'tbl_1': 8.0,
     'tbl_2': 8.0,
     'tbl_3': 8.0,
     'tbl_4': 8.0,
     'tbl_5': 8.0,
     'tbl_6': 8.0,
     'tbl_7': 8.0,
     'tbl_8': 8.0,
     'tbl_9': 8.0,
     'tbl_10': 8.0,
     'tbl_11': 8.0,
     'tbl_12': 8.0,
     'tbl_13': 8.0,
     'tbl_14': 8.0,
     'tbl_15': 8.0,
     'tbl_16': 8.0,
     'tbl_17': 8.0,
     'tbl_18': 8.0,
     'tbl_19': 8.0,
     'tbl_20': 8.0,
     'tbl_21': 7.69,
     'tbl_22': 8.0,
     'tbl_23': 8.0,
     'tbl_24': 8.0,
     'tbl_25': 8.0,
     'L0_rec_W1': 7.893,
     'L0_rec_W2': 3.924,
     'dense_ctx': 5.185}
    for name, (base, spread) in spreads.items():
        noise = np.random.default_rng([zlib.crc32(name.encode()), seed]).standard_normal(out[name].shape)
        drawn = base * np.exp(spread * noise) if base else spread * noise
        out[name] = jnp.asarray(drawn.astype(out[name].dtype))
    for name, factor in factors.items():
        out[name] = (out[name] * factor).astype(out[name].dtype)
    return out
```

```python
import concourse.bass as bass
from concourse import mybir
from concourse.alu_op_type import AluOpType as ALU
from contextlib import ExitStack

FIELDS, K, BATCH, HID = 26, 32, 512, 128
CHUNK = 128
CHUNKS = BATCH // CHUNK
QUADS = 4
GROUPS = CHUNK // QUADS
STARTS, SIZES = (0, 8, 17), (8, 9, 9)
D, E, F = 0, 1, 2
PARTS = (E, F, D)
ND, NE, NF = SIZES
TRI = [n * (n + 1) // 2 for n in SIZES]
ROWS_AT = (0, TRI[0], TRI[0] + TRI[1])
ONE = sum(TRI)
NY = ONE + 1
NEF = NE * NF
NX = NEF + NE + NF
CY = FIELDS + 1
CX = ND + 1
PCOLS = NY + NX
CROSS = 225
RCOLS = NY + CROSS
YB, XB = 4, 8
U1, U2 = 512, 256


def shift_row(part, s):
    return ROWS_AT[part] + sum(SIZES[part] - t for t in range(s))


def tower_kernel(nc, dense_t, ids, tables, w_top1, b_top1, w_top2, b_top2, w_top3, w1, b1, w2t, b2, out):
    f32, i32 = mybir.dt.float32, mybir.dt.int32
    ACT = mybir.ActivationFunctionType
    assert NY <= 128 and NX <= 128 and NEF + ND * (NE + NF) == CROSS == NE * (ND + NF) + NF * ND

    with ExitStack() as ctx:
        def sb(name, shape, dt=f32):
            return ctx.enter_context(nc.sbuf_tensor(name, shape, dt))

        def sem(name):
            return ctx.enter_context(nc.semaphore(name))

        def view(t, offset, dims, at=0, parts=128):
            row = 1
            for n in t.shape[1:]:
                row *= n
            return bass.AP(t, at * row + offset, [[row, parts]] + [list(d) for d in dims])

        ids_all = sb("ids_all", [128, CHUNKS, FIELDS], i32)
        ids_now = sb("ids_now", [128, FIELDS], i32)
        rows = sb("rows", [128, FIELDS, K])
        emb = sb("emb", [128, GROUPS, FIELDS])
        blk = sb("blk", [128, GROUPS, QUADS, CY])
        prod = sb("prod", [128, GROUPS, PCOLS])
        t_y = sb("t_y", [NY, CY, CHUNK])
        t_x = sb("t_x", [NX, CX, CHUNK])
        w1_raw = sb("w1_raw", [128, FIELDS, FIELDS])
        wq = sb("wq", [128, FIELDS, FIELDS])
        w2 = sb("w2", [128, FIELDS, HID])
        wq_y = sb("wq_y", [128, NY])
        wq_cross = sb("wq_cross", [128, 3, CROSS])
        wq_x = sb("wq_x", [128, CX, NX])
        r = sb("r", [128, FIELDS, RCOLS])
        v_y = sb("v_y", [NY, FIELDS, HID])
        v_x = sb("v_x", [NEF, ND, HID])
        u_y = sb("u_y", [NY, HID])
        u_x = sb("u_x", [NX, CX, HID])
        ident = sb("ident", [128, 128])
        b2_col = sb("b2_col", [128, 1])
        kb2 = sb("kb2", [128, 1])
        z = sb("z", [128, 2, CHUNK])
        dense = sb("dense", [16, BATCH])
        wt1 = sb("wt1", [128, 2, U1])
        wt1d = sb("wt1d", [16, U1])
        bt1 = sb("bt1", [128, U1 // 128])
        wt2 = sb("wt2", [128, U1 // 128, U2])
        bt2 = sb("bt2", [128, U2 // 128])
        wt3 = sb("wt3", [128, U2 // 128])
        h1 = sb("h1", [128, U1 // 128, CHUNK])
        h2 = sb("h2", [128, U2 // 128, CHUNK])
        y = sb("y", [1, BATCH])

        bank = [ctx.enter_context(nc.psum_tensor(f"bank{n}", [128, 512], f32)) for n in range(8)]
        ps_y, ps_x = bank[0:2], bank[2:4]
        ps_z = bank[4:6]
        ps_h1, ps_h2 = bank[6], bank[7]
        ps_out = ps_h2[:, U2:U2 + CHUNK]

        ids_loaded, w1_loaded, w2_loaded, b1_loaded = sem("ids_loaded"), sem("w1_loaded"), sem("w2_loaded"), sem("b1_loaded")
        mlp_loaded, b2_loaded = sem("mlp_loaded"), sem("b2_loaded")
        ids_copied = sem("ids_copied")
        rows_in = [sem(f"rows_in{p}") for p in range(3)]
        rows_used = [sem(f"rows_used{p}") for p in range(3)]
        blk_copied = sem("blk_copied")
        presets = sem("presets")
        ident_ready = sem("ident_ready")
        dve_done = sem("dve_done")
        wq_ready = sem("wq_ready")
        cross_mm, cross_out = sem("cross_mm"), sem("cross_out")
        cross_added = sem("cross_added")
        turned, turned_out = sem("turned"), sem("turned_out")
        kb2_ready = sem("kb2_ready")
        prod_ready = sem("prod_ready")
        y_mm, x_mm = sem("y_mm"), sem("x_mm")
        y_out, x_out = sem("y_out"), sem("x_out")
        z2_mm, z1_mm, z2_out, z1_out = sem("z2_mm"), sem("z1_mm"), sem("z2_out"), sem("z1_out")
        h1_mm, h1_out, h2_mm, h2_out = sem("h1_mm"), sem("h1_out"), sem("h2_mm"), sem("h2_out")
        out_mm, out_out, stored = sem("out_mm"), sem("out_out"), sem("stored")

        NYB, NXB = GROUPS // YB, GROUPS // XB
        TURN_U = [("uy", 0, 1)] + [("ux", n, min(4, CX - n)) for n in range(0, CX, 4)]
        TURN_V = [("vx", n, 4) for n in range(0, ND, 4)] + [("vy", n, min(4, FIELDS - n)) for n in range(0, FIELDS, 4)]
        U1T, U2T = U1 // 128, U2 // 128
        CROSS_BANKS = 6

        block = ctx.enter_context(nc.Block())

        @block.sync
        def _(sp):
            sp.dma_start(ids_all[:, :, :], ids.rearrange("(c p) f -> p c f", p=CHUNK)).then_inc(ids_loaded, 16)
            sp.dma_start(w1_raw[:, :, :], w1).then_inc(w1_loaded, 16)
            half = FIELDS // 2
            sp.dma_start(w2[:, 0:half, :], w2t[:, 0:half, :]).then_inc(w2_loaded, 16)
            sp.dma_start(w2[:, half:, :], w2t[:, half:, :]).then_inc(w2_loaded, 16)
            sp.dma_start(wt1[:, :, :], w_top1[0:2 * HID, :].rearrange("(t p) n -> p t n", p=128)).then_inc(mlp_loaded, 16)
            sp.dma_start(wt1d[:, :], w_top1[2 * HID:, :]).then_inc(mlp_loaded, 16)
            sp.dma_start(dense[:, :], dense_t).then_inc(mlp_loaded, 16)
            sp.dma_start(wt2[:, :, :], w_top2.rearrange("(t p) n -> p t n", p=128)).then_inc(mlp_loaded, 16)
            sp.dma_start(bt1[:, :], b_top1).then_inc(mlp_loaded, 16)
            sp.dma_start(bt2[:, :], b_top2).then_inc(mlp_loaded, 16)
            sp.dma_start(wt3[:, :], w_top3).then_inc(mlp_loaded, 16)
            sp.wait_ge(out_out, CHUNKS)
            sp.dma_start(out, y[:, :]).then_inc(stored, 16)
            sp.wait_ge(stored, 16)
        MLP_LOADS = 7 * 16

        @block.gpsimd
        def _(pool):
            pool.memset(ident[:, :], 0.0).then_inc(ident_ready, 1)
            pool.wait_ge(ident_ready, 1)
            pool.affine_select(out=ident[:, :], in_=ident[:, :], compare_op=ALU.not_equal, fill=1.0, base=0,
                               pattern=[[-1, 128]], channel_multiplier=1).then_inc(ident_ready, 1)
            pool.wait_ge(ids_loaded, 16)

            def gather(c, first):
                for n, p in enumerate(PARTS):
                    at, size = STARTS[p], SIZES[p]
                    if not first:
                        pool.wait_ge(rows_used[p], c)
                    pool.tensor_copy(ids_now[:, at:at + size], ids_all[:, c, at:at + size]).then_inc(ids_copied, 1)
                    pool.wait_ge(ids_copied, 3 * c + n + 1)
                    pool.nop(nofuse=True)
                    for f in range(at, at + size):
                        pool.indirect_dma_start(
                            rows[:, f, :], None, tables[f],
                            bass.IndirectOffsetOnAxis(ap=ids_now[:, f:f + 1], axis=0)).then_inc(rows_in[p], 16)

            gather(0, True)
            with pool.Fori(1, CHUNKS) as c:
                gather(c, False)

        def diagonal(part, s):
            return view(wq, STARTS[part] * (FIELDS + 1) + s, [(FIELDS + 1, SIZES[part] - s)])

        @block.vector
        def _(dve):
            steps = [0]

            def settle(instruction):
                steps[0] += 1
                instruction.then_inc(dve_done, 1)
                dve.wait_ge(dve_done, steps[0])

            dve.memset(wq_x[:, :, :], 0.0)
            settle(dve.memset(blk[:, :, :, :], 0.0))
            for q in range(QUADS):
                dve.memset(blk[32 * q:32 * q + 32, :, q, 0:1], 1.0)
            dve.memset(prod[:, :, ONE:ONE + 1], 1.0).then_inc(presets, 1)

            dve.wait_ge(w1_loaded, 16)
            settle(dve.tensor_tensor(wq[:, :, :], w1_raw[:, :, :], w1_raw[:, :, :].rearrange("p a b -> p b a"), ALU.add))
            settle(dve.tensor_copy(view(wq, 0, [(FIELDS + 1, FIELDS)]), view(w1_raw, 0, [(FIELDS + 1, FIELDS)])))
            d0, e0, f0 = STARTS
            for p in range(3):
                for s in range(SIZES[p]):
                    at = shift_row(p, s)
                    dve.tensor_copy(wq_y[:, at:at + SIZES[p] - s], diagonal(p, s))

            def block_of(out_t, offset, a0, na, c0, nc_):
                step = nc_
                if isinstance(offset, tuple):
                    offset, step = offset
                return dve.tensor_copy(view(out_t, offset, [(step, na), (1, nc_)]), wq[:, a0:a0 + na, c0:c0 + nc_])

            block_of(wq_cross, 0, e0, NE, f0, NF)
            block_of(wq_cross, NEF, d0, ND, e0, NE + NF)
            block_of(wq_cross, (CROSS, ND + NF), e0, NE, d0, ND)
            block_of(wq_cross, (CROSS + ND, ND + NF), e0, NE, f0, NF)
            block_of(wq_cross, CROSS + NE * (ND + NF), f0, NF, d0, ND)
            block_of(wq_cross, 2 * CROSS, f0, NF, d0, ND + NE)
            block_of(wq_cross, 2 * CROSS + NF * (ND + NE), e0, NE, d0, ND).then_inc(wq_ready, 1)
            block_of(wq_x, 0, e0, NE, f0, NF)
            dve.tensor_copy(view(wq_x, NX + NEF, [(NX, ND), (1, NE + NF)]),
                            wq[:, e0:, 0:ND].rearrange("p i j -> p j i")).then_inc(wq_ready, 1)

            def products(c, first):
                for p in PARTS:
                    at, size = STARTS[p], SIZES[p]
                    dve.wait_ge(rows_in[p], 16 * size * (c + 1))
                    if not first:
                        dve.wait_ge(blk_copied, 3 * c)
                    dve.transpose(emb[:, :, at:at + size].rearrange("p g f -> p f g"),
                                  rows[:, at:at + size, :]).then_inc(rows_used[p], 1)
                    dve.wait_ge(rows_used[p], c + 1)
                    if p == PARTS[0] and not first:
                        dve.wait_ge(x_mm, NXB * c)
                    for s in range(size):
                        row = shift_row(p, s)
                        last = dve.tensor_tensor(prod[:, :, row:row + size - s], emb[:, :, at:at + size - s],
                                                 emb[:, :, at + s:at + size], ALU.mult)
                    if p == F:
                        one_f = [(FIELDS, GROUPS), (0, NE), (1, NF)]
                        e_one = [(FIELDS, GROUPS), (1, NE), (0, NF)]
                        dve.tensor_tensor(view(prod, NY, [(PCOLS, GROUPS), (NF, NE), (1, NF)]),
                                          view(emb, e0, e_one), view(emb, f0, one_f), ALU.mult)
                        dve.tensor_copy(prod[:, :, NY + NEF:], emb[:, :, e0:])
                last.then_inc(prod_ready, 1)

            products(0, True)

            dve.wait_ge(cross_out, FIELDS)
            other, single = NY, NY + NEF
            wide = ND + NE

            def add_cross(which):
                for s in range(which, ND):
                    rows_at = shift_row(D, s)
                    dst = view(r, e0 * RCOLS + rows_at, [(1, ND - s), (RCOLS, NE + NF)])
                    src = single + ((s * RCOLS) if which == 0 else s * (NE + NF))
                    dve.tensor_tensor(dst, dst, view(r, src, [(RCOLS + NE + NF, ND - s), (1, NE + NF)]), ALU.add)
                for p, o in ((E, F), (F, E)):
                    for s in range(which, SIZES[p]):
                        rows_at = shift_row(p, s)
                        src = STARTS[p] * RCOLS + other + ((s * RCOLS) if which == 0 else s * wide)
                        for c0, n, slot in ((0, ND, 0), (STARTS[o], SIZES[o], ND)):
                            dst = view(r, c0 * RCOLS + rows_at, [(1, SIZES[p] - s), (RCOLS, n)])
                            dve.tensor_tensor(dst, dst, view(r, src + slot, [(RCOLS + wide, SIZES[p] - s), (1, n)]), ALU.add)
                dst = view(r, NY, [(NF, NE), (1, NF), (RCOLS, ND)])
                tail = NY + NE * wide
                if which == 0:
                    src = view(r, f0 * RCOLS + tail, [(ND, NE), (RCOLS, NF), (1, ND)])
                else:
                    src = view(r, e0 * RCOLS + tail, [(RCOLS, NE), (ND, NF), (1, ND)])
                return dve.tensor_tensor(dst, dst, src, ALU.add)

            settle(add_cross(0))
            add_cross(1).then_inc(cross_added, 1)

            with dve.Fori(1, CHUNKS) as c:
                products(c, False)

        @block.scalar
        def _(act):
            act.dma_start(wq_y[:, ONE:ONE + 1], b1).then_inc(b1_loaded, 16)
            act.dma_start(b2_col[:, :], b2).then_inc(b2_loaded, 16)
            act.wait_ge(b2_loaded, 16)
            act.activation(kb2[:, :], b2_col[:, :], ACT.Copy, scale=float(K)).then_inc(kb2_ready, 1)
            act.wait_ge(kb2_ready, 1)
            for c in range(FIELDS):
                act.wait_ge(cross_mm, c + 1)
                act.activation(r[:, c, :], bank[c % CROSS_BANKS][:, 0:RCOLS], ACT.Copy).then_inc(cross_out, 1)

            def turn_out(turns, first):
                for n, (what, c0, m) in enumerate(turns):
                    dst = {"uy": u_y, "ux": u_x, "vx": v_x, "vy": v_y}[what]
                    src = bank[(first + n) % 8]
                    act.wait_ge(turned, first + n + 1)
                    if what == "uy":
                        ins = act.activation(u_y[:, :], src[0:NY, 0:HID], ACT.Copy)
                    else:
                        ins = act.activation(dst[:, c0:c0 + m, :].rearrange("p c h -> p (c h)"),
                                             src[0:dst.shape[0], 0:m * HID], ACT.Copy)
                    ins.then_inc(turned_out, 1)

            def blk_copy(c, first):
                for n, p in enumerate(PARTS):
                    at, size = STARTS[p], SIZES[p]
                    act.wait_ge(rows_used[p], c + 1)
                    if n == 0 and not first:
                        act.wait_ge(x_mm, NXB * c)
                    for q in range(QUADS):
                        ins = act.activation(blk[32 * q:32 * q + 32, :, q, 1 + at:1 + at + size],
                                             emb[32 * q:32 * q + 32, :, at:at + size], ACT.Copy)
                    ins.then_inc(blk_copied, 1)

            def t_out(c):
                for n in range(NYB):
                    act.wait_ge(y_mm, NYB * c + n + 1)
                    act.activation(
                        view(t_y, n * YB, [(32, QUADS), (CHUNK, CY), (1, YB)], parts=NY),
                        view(ps_y[n % 2], 0, [(CY, QUADS), (1, CY), (QUADS * CY, YB)], parts=NY),
                        ACT.Copy).then_inc(y_out, 1)
                    if n % 2 == 1:
                        m = n // 2
                        act.wait_ge(x_mm, NXB * c + m + 1)
                        act.activation(
                            view(t_x, m * XB, [(32, QUADS), (CHUNK, CX), (1, XB)], parts=NX),
                            view(ps_x[m % 2], 0, [(CX, QUADS), (1, CX), (QUADS * CX, XB)], parts=NX),
                            ACT.Copy).then_inc(x_out, 1)

            def z_out(c, which, mm, done, bias):
                act.wait_ge(mm, c + 1)
                if bias is None:
                    act.activation(z[:, which, :], ps_z[which][:, 0:CHUNK], ACT.Copy).then_inc(done, 1)
                else:
                    act.activation(z[:, which, :], ps_z[which][:, 0:CHUNK], ACT.Identity, bias=bias).then_inc(done, 1)

            def h1_relu(c):
                act.wait_ge(h1_mm, c + 1)
                for t in range(U1T):
                    ins = act.activation(h1[:, t, :], ps_h1[:, t * CHUNK:(t + 1) * CHUNK], ACT.Relu, bias=bt1[:, t:t + 1])
                ins.then_inc(h1_out, 1)

            def h2_relu(c):
                act.wait_ge(h2_mm, c + 1)
                for t in range(U2T):
                    ins = act.activation(h2[:, t, :], ps_h2[:, t * CHUNK:(t + 1) * CHUNK], ACT.Relu, bias=bt2[:, t:t + 1])
                ins.then_inc(h2_out, 1)

            def out_copy(c):
                act.wait_ge(out_mm, c + 1)
                act.activation(y[0:1, bass.ts(c, CHUNK)], ps_out[0:1, :], ACT.Copy).then_inc(out_out, 1)

            def chunk(c, first, last):
                t_out(c)
                if not first:
                    h1_relu(c - 1)
                if not last:
                    blk_copy(c + 1, False)
                if first:
                    turn_out(TURN_V, len(TURN_U))
                z_out(c, 1, z2_mm, z2_out, kb2[:, 0:1])
                if not first:
                    h2_relu(c - 1)
                z_out(c, 0, z1_mm, z1_out, None)
                if not first:
                    out_copy(c - 1)

            act.wait_ge(presets, 1)
            blk_copy(0, True)
            turn_out(TURN_U, 0)
            act.wait_ge(mlp_loaded, MLP_LOADS)
            chunk(0, True, False)
            with act.Fori(1, CHUNKS - 1) as c:
                chunk(c, False, False)
            chunk(CHUNKS - 1, False, True)
            h1_relu(CHUNKS - 1)
            h2_relu(CHUNKS - 1)
            out_copy(CHUNKS - 1)

        @block.tensor
        def _(pe):
            part_of = [p for p in range(3) for _ in range(SIZES[p])]
            pe.wait_ge(wq_ready, 1)
            pe.wait_ge(w2_loaded, 32)
            pe.wait_ge(b1_loaded, 16)
            for c in range(FIELDS):
                if c >= CROSS_BANKS:
                    pe.wait_ge(cross_out, c - CROSS_BANKS + 1)
                ps = bank[c % CROSS_BANKS]
                pe.matmul(ps[:, 0:NY], w2[:, c, :], wq_y[:, :], start=True, stop=True)
                pe.matmul(ps[:, NY:RCOLS], w2[:, c, :], wq_cross[:, part_of[c], :], start=True, stop=True).then_inc(cross_mm, 1)

            def turn(turns, first):
                for n, (what, c0, m) in enumerate(turns):
                    if first + n >= 8:
                        pe.wait_ge(turned_out, first + n - 7)
                    ps = bank[(first + n) % 8]
                    for j in range(m):
                        src = {"uy": wq_y[:, :], "ux": wq_x[:, min(c0 + j, CX - 1), :],
                               "vx": r[:, c0 + j, NY:NY + NEF], "vy": r[:, c0 + j, 0:NY]}[what]
                        ins = pe.transpose(ps[0:src.shape[1], j * HID:(j + 1) * HID], src, ident[:, :])
                    ins.then_inc(turned, 1)

            def t_matmuls(c, first):
                pe.wait_ge(prod_ready, c + 1)
                pe.wait_ge(blk_copied, 3 * (c + 1))
                for n in range(NYB):
                    if not first or n >= 2:
                        pe.wait_ge(y_out, NYB * c + n - 1)
                    for j in range(YB):
                        g = n * YB + j
                        ins = pe.matmul(ps_y[n % 2][0:NY, j * QUADS * CY:(j + 1) * QUADS * CY], prod[:, g, 0:NY],
                                        blk[:, g, :, :].rearrange("p q c -> p (q c)"), start=True, stop=True)
                    ins.then_inc(y_mm, 1)
                    if n % 2 == 1:
                        m = n // 2
                        if not first or m >= 2:
                            pe.wait_ge(x_out, NXB * c + m - 1)
                        for j in range(XB):
                            g = m * XB + j
                            ins = pe.matmul(ps_x[m % 2][0:NX, j * QUADS * CX:(j + 1) * QUADS * CX], prod[:, g, NY:],
                                            blk[:, g, :, 0:CX], start=True, stop=True)
                        ins.then_inc(x_mm, 1)

            def z2_matmuls(c, first):
                pe.wait_ge(y_out, NYB * (c + 1))
                pe.wait_ge(x_out, NXB * (c + 1))
                if not first:
                    pe.wait_ge(z2_out, c)
                for j in range(ND):
                    pe.matmul(ps_z[1][:, 0:CHUNK], v_x[:, j, :], t_x[0:NEF, 1 + j, :], start=(j == 0), stop=False)
                for j in range(FIELDS):
                    ins = pe.matmul(ps_z[1][:, 0:CHUNK], v_y[:, j, :], t_y[:, 1 + j, :], start=False, stop=(j == FIELDS - 1))
                ins.then_inc(z2_mm, 1)

            def z1_matmuls(c, first):
                if not first:
                    pe.wait_ge(z1_out, c)
                pe.matmul(ps_z[0][:, 0:CHUNK], u_y[:, :], t_y[:, 0, :], start=True, stop=False)
                for j in range(CX):
                    ins = pe.matmul(ps_z[0][:, 0:CHUNK], u_x[:, j, :], t_x[:, j, :], start=False, stop=(j == CX - 1))
                ins.then_inc(z1_mm, 1)

            def mlp1(c):
                pe.wait_ge(z1_out, c + 1)
                pe.wait_ge(z2_out, c + 1)
                for t in range(U1T):
                    ps = ps_h1[:, t * CHUNK:(t + 1) * CHUNK]
                    pe.matmul(ps, wt1d[:, t * 128:(t + 1) * 128], dense[:, bass.ts(c, CHUNK)], start=True, stop=False)
                    for k in range(2):
                        ins = pe.matmul(ps, wt1[:, k, t * 128:(t + 1) * 128], z[:, k, :], start=False, stop=(k == 1))
                ins.then_inc(h1_mm, 1)

            def mlp2(c):
                pe.wait_ge(h1_out, c + 1)
                for t in range(U2T):
                    for k in range(U1T):
                        ins = pe.matmul(ps_h2[:, t * CHUNK:(t + 1) * CHUNK], wt2[:, k, t * 128:(t + 1) * 128],
                                        h1[:, k, :], start=(k == 0), stop=(k == U1T - 1))
                ins.then_inc(h2_mm, 1)

            def mlp3(c):
                pe.wait_ge(h2_out, c + 1)
                for k in range(U2T):
                    ins = pe.matmul(ps_out[0:1, :], wt3[:, k:k + 1], h2[:, k, :], start=(k == 0), stop=(k == U2T - 1))
                ins.then_inc(out_mm, 1)

            def chunk(c):
                t_matmuls(c, False)
                mlp1(c - 1)
                z2_matmuls(c, False)
                mlp2(c - 1)
                z1_matmuls(c, False)
                mlp3(c - 1)

            pe.wait_ge(cross_out, FIELDS)
            pe.wait_ge(ident_ready, 2)
            pe.wait_ge(wq_ready, 2)
            turn(TURN_U, 0)
            pe.wait_ge(turned_out, len(TURN_U))
            t_matmuls(0, True)
            pe.wait_ge(cross_added, 1)
            pe.wait_ge(y_out, NYB)
            pe.wait_ge(x_out, NXB)
            turn(TURN_V, len(TURN_U))
            pe.wait_ge(turned_out, len(TURN_U) + len(TURN_V))
            pe.wait_ge(mlp_loaded, MLP_LOADS)
            z2_matmuls(0, True)
            z1_matmuls(0, True)
            with pe.Fori(1, CHUNKS) as c:
                chunk(c)
            mlp1(CHUNKS - 1)
            mlp2(CHUNKS - 1)
            mlp3(CHUNKS - 1)


def kernel(**inputs):
    import numpy as np
    import concourse.bacc as bacc
    from concourse.bass_utils import run_bass_kernel_spmd

    nc = bacc.Bacc("TRN2", target_bir_lowering=False, num_devices=1)
    laid_out = {
        "dense_t": np.ascontiguousarray(np.transpose(inputs["dense_ctx"])),
        "ids": np.ascontiguousarray(inputs["ids"]),
        "w_top1": np.ascontiguousarray(inputs["W_top1"]),
        "b_top1": np.ascontiguousarray(np.transpose(np.reshape(inputs["b_top1"], (4, 128)))),
        "w_top2": np.ascontiguousarray(inputs["W_top2"]),
        "b_top2": np.ascontiguousarray(np.transpose(np.reshape(inputs["b_top2"], (2, 128)))),
        "w_top3": np.ascontiguousarray(np.transpose(np.reshape(inputs["W_top3"], (2, 128)))),
        "w1": np.ascontiguousarray(inputs["L0_rec_W1"]),
        "b1": np.ascontiguousarray(np.reshape(inputs["L0_rec_b1"], (128, 1))),
        "w2t": np.ascontiguousarray(np.transpose(inputs["L0_rec_W2"], (1, 2, 0))),
        "b2": np.ascontiguousarray(np.reshape(inputs["L0_rec_b2"], (128, 1))),
    }
    for f in range(FIELDS):
        laid_out[f"tbl_{f}"] = np.ascontiguousarray(inputs[f"tbl_{f}"])
    dram = {name: nc.dram_tensor(name, a.shape, mybir.dt.from_np(a.dtype), kind="ExternalInput").ap()
            for name, a in laid_out.items()}
    out = nc.dram_tensor("scores", (1, BATCH), mybir.dt.float32, kind="ExternalOutput").ap()
    tower_kernel(nc, dram["dense_t"], dram["ids"], [dram[f"tbl_{f}"] for f in range(FIELDS)],
                 dram["w_top1"], dram["b_top1"], dram["w_top2"], dram["b_top2"], dram["w_top3"],
                 dram["w1"], dram["b1"], dram["w2t"], dram["b2"], out)
    result = run_bass_kernel_spmd(nc, [laid_out], core_ids=[0])
    return np.reshape(result.results[0]["scores"], (BATCH, 1))
```

```python
import concourse.bass as bass
from concourse import mybir
from concourse.alu_op_type import AluOpType as ALU
from contextlib import ExitStack

FIELDS, K, BATCH, HID = 26, 32, 512, 128
CHUNK = 128
CHUNKS = BATCH // CHUNK
QUADS = 4
GROUPS = CHUNK // QUADS
STARTS, SIZES = (0, 8, 17), (8, 9, 9)
D, E, F = 0, 1, 2
PARTS = (E, F, D)
ND, NE, NF = SIZES
TRI = [n * (n + 1) // 2 for n in SIZES]
ROWS_AT = (0, TRI[0], TRI[0] + TRI[1])
ONE = sum(TRI)
NY = ONE + 1
NEF = NE * NF
NX = NEF + NE + NF
CY = FIELDS + 1
CX = ND + 1
PCOLS = NY + NX
MROWS = ND * (NE + NF) // 2
CROSS = 225
RCOLS = NY + CROSS
WRAP = (3, 4, 4)
EMB_AT = (0, 11, 24)
EMB_COLS = FIELDS + sum(WRAP)
YB, XB = 4, 8
U1, U2 = 512, 256


def shift_row(part, s):
    n = SIZES[part]
    return ROWS_AT[part] + (s * n if s <= n // 2 else (n - s) * n + s)


def tower_kernel(nc, dense_t, ids, tables, w_top1, b_top1, w_top2, b_top2, w_top3, w1, b1, w2t, b2, out):
    f32, i32 = mybir.dt.float32, mybir.dt.int32
    ACT = mybir.ActivationFunctionType
    assert NY <= 128 and NX <= 128 and NEF + ND * (NE + NF) == CROSS == NE * (ND + NF) + NF * ND

    with ExitStack() as ctx:
        def sb(name, shape, dt=f32):
            return ctx.enter_context(nc.sbuf_tensor(name, shape, dt))

        def sem(name):
            return ctx.enter_context(nc.semaphore(name))

        def view(t, offset, dims, at=0, parts=128):
            row = 1
            for n in t.shape[1:]:
                row *= n
            return bass.AP(t, at * row + offset, [[row, parts]] + [list(d) for d in dims])

        ids_all = sb("ids_all", [128, CHUNKS, FIELDS], i32)
        rows = sb("rows", [128, FIELDS, K])
        emb = sb("emb", [128, GROUPS, EMB_COLS])
        blk = sb("blk", [128, GROUPS, QUADS, CY])
        prod = sb("prod", [128, GROUPS, PCOLS])
        t_y = sb("t_y", [NY, CY, CHUNK])
        t_x = sb("t_x", [NX, CX, CHUNK])
        w1_raw = sb("w1_raw", [128, FIELDS, FIELDS])
        wq = sb("wq", [128, FIELDS, FIELDS])
        w2 = sb("w2", [128, FIELDS, HID])
        wq_y = sb("wq_y", [128, NY])
        wq_cross = sb("wq_cross", [128, 3, CROSS])
        r = sb("r", [128, FIELDS, RCOLS])
        v_y = sb("v_y", [NY, FIELDS, HID])
        v_x = sb("v_x", [NEF, ND, HID])
        u_y = sb("u_y", [NY, HID])
        u_x = sb("u_x", [NEF, HID])
        u_m = sb("u_m", [MROWS, 2, HID])
        m_x = sb("m_x", [MROWS, 2, CHUNK])
        ident = sb("ident", [128, 128])
        b2_col = sb("b2_col", [128, 1])
        kb2 = sb("kb2", [128, 1])
        z = sb("z", [128, 2, CHUNK])
        dense = sb("dense", [16, BATCH])
        wt1 = sb("wt1", [128, 2, U1])
        wt1d = sb("wt1d", [16, U1])
        bt1 = sb("bt1", [128, U1 // 128])
        wt2 = sb("wt2", [128, U1 // 128, U2])
        bt2 = sb("bt2", [128, U2 // 128])
        wt3 = sb("wt3", [128, U2 // 128])
        h1 = sb("h1", [128, U1 // 128, CHUNK])
        h2 = sb("h2", [128, U2 // 128, CHUNK])
        y = sb("y", [1, BATCH])

        bank = [ctx.enter_context(nc.psum_tensor(f"bank{n}", [128, 512], f32)) for n in range(8)]
        ps_y, ps_x = bank[0:2], bank[2:4]
        ps_z = bank[4:6]
        ps_h1 = (bank[6], bank[7], bank[4], bank[5])
        ps_h2, ps_out = (bank[6], bank[7]), bank[4]

        ids_loaded, w1_loaded, w2_loaded, b1_loaded = sem("ids_loaded"), sem("w1_loaded"), sem("w2_loaded"), sem("b1_loaded")
        mlp_loaded, b2_loaded = sem("mlp_loaded"), sem("b2_loaded")
        rows_in = [sem(f"rows_in{p}") for p in range(3)]
        rows_used = [sem(f"rows_used{p}") for p in range(3)]
        presets = sem("presets")
        ident_ready = sem("ident_ready")
        dve_done = sem("dve_done")
        wq_ready = sem("wq_ready")
        cross_mm, cross_out = sem("cross_mm"), sem("cross_out")
        cross_added = sem("cross_added")
        turned, turned_out = sem("turned"), sem("turned_out")
        kb2_ready = sem("kb2_ready")
        pairs_ready = sem("pairs_ready")
        blk_copied = sem("blk_copied")
        prod_ready = sem("prod_ready")
        y_mm, x_mm = sem("y_mm"), sem("x_mm")
        y_out, x_out = sem("y_out"), sem("x_out")
        z2_mm, z1_mm, z2_out, z1_out = sem("z2_mm"), sem("z1_mm"), sem("z2_out"), sem("z1_out")
        m_moved = sem("m_moved")
        h1_mm, h1_out, h2_mm, h2_out = sem("h1_mm"), sem("h1_out"), sem("h2_mm"), sem("h2_out")
        out_mm, out_out, stored = sem("out_mm"), sem("out_out"), sem("stored")

        NYB, NXB = GROUPS // YB, GROUPS // XB
        TURN_U = [("uxy", 0, 2), ("um", 0, 2)]
        TURN_V = [("vy", n, min(4, FIELDS - n)) for n in range(0, FIELDS, 4)] + [("vx", n, 4) for n in range(0, ND, 4)]
        U1T, U2T = U1 // 128, U2 // 128
        CROSS_BANKS = 6
        TURN_BANKS = (6, 7) + (5, 4, 6, 7, 0, 1, 2, 3, 4)
        GATED = 5

        block = ctx.enter_context(nc.Block())

        @block.sync
        def _(sp):
            sp.dma_start(ids_all[:, :, :], ids.rearrange("(c p) f -> p c f", p=CHUNK)).then_inc(ids_loaded, 16)
            sp.dma_start(w1_raw[:, :, :], w1).then_inc(w1_loaded, 16)
            half = FIELDS // 2
            sp.dma_start(w2[:, 0:half, :], w2t[:, 0:half, :]).then_inc(w2_loaded, 16)
            sp.dma_start(w2[:, half:, :], w2t[:, half:, :]).then_inc(w2_loaded, 16)
            sp.dma_start(wt1[:, :, :], w_top1[0:2 * HID, :].rearrange("(t p) n -> p t n", p=128)).then_inc(mlp_loaded, 16)
            sp.dma_start(wt1d[:, :], w_top1[2 * HID:, :]).then_inc(mlp_loaded, 16)
            sp.dma_start(dense[:, :], dense_t).then_inc(mlp_loaded, 16)
            sp.dma_start(wt2[:, :, :], w_top2.rearrange("(t p) n -> p t n", p=128)).then_inc(mlp_loaded, 16)
            sp.dma_start(bt1[:, :], b_top1).then_inc(mlp_loaded, 16)
            sp.dma_start(bt2[:, :], b_top2).then_inc(mlp_loaded, 16)
            sp.dma_start(wt3[:, :], w_top3).then_inc(mlp_loaded, 16)
            def move_m(c, first):
                sp.wait_ge(x_out, NXB * (c + 1))
                if not first:
                    sp.wait_ge(z1_mm, c)
                for n in range(2):
                    for j in range(ND // 2):
                        sp.dma_start(m_x[j * (NE + NF):(j + 1) * (NE + NF), n, :],
                                     t_x[NEF:, 1 + n * ND // 2 + j, :]).then_inc(m_moved, 16)

            move_m(0, True)
            with sp.Fori(1, CHUNKS) as c:
                move_m(c, False)
            sp.wait_ge(out_out, CHUNKS)
            sp.dma_start(out, y[:, :]).then_inc(stored, 16)
            sp.wait_ge(stored, 16)
        MLP_LOADS = 7 * 16

        @block.gpsimd
        def _(pool):
            pool.memset(ident[:, :], 0.0).then_inc(ident_ready, 1)
            pool.wait_ge(ident_ready, 1)
            pool.affine_select(out=ident[:, :], in_=ident[:, :], compare_op=ALU.not_equal, fill=1.0, base=0,
                               pattern=[[-1, 128]], channel_multiplier=1).then_inc(ident_ready, 1)
            pool.wait_ge(ids_loaded, 16)

            for c in range(CHUNKS):
                for p in PARTS:
                    if c > 0:
                        pool.wait_ge(rows_used[p], c)
                    for f in range(STARTS[p], STARTS[p] + SIZES[p]):
                        pool.indirect_dma_start(
                            rows[:, f, :], None, tables[f],
                            bass.IndirectOffsetOnAxis(ap=ids_all[:, c, f:f + 1], axis=0)).then_inc(rows_in[p], 16)

        def diagonal(part, s):
            return view(wq, STARTS[part] * (FIELDS + 1) + s, [(FIELDS + 1, SIZES[part] - s)])

        def blk_views(p, q):
            here = slice(32 * q, 32 * q + 32)
            return (blk[here, :, q, 1 + STARTS[p]:1 + STARTS[p] + SIZES[p]],
                    emb[here, :, EMB_AT[p]:EMB_AT[p] + SIZES[p]])

        @block.vector
        def _(dve):
            steps = [0]

            def settle(instruction):
                steps[0] += 1
                instruction.then_inc(dve_done, 1)
                dve.wait_ge(dve_done, steps[0])

            dve.wait_ge(w1_loaded, 16)
            settle(dve.tensor_tensor(wq[:, :, :], w1_raw[:, :, :], w1_raw[:, :, :].rearrange("p a b -> p b a"), ALU.add))
            settle(dve.tensor_copy(view(wq, 0, [(FIELDS + 1, FIELDS)]), view(w1_raw, 0, [(FIELDS + 1, FIELDS)])))
            d0, e0, f0 = STARTS
            for p in range(3):
                for s in range(SIZES[p]):
                    at = shift_row(p, s)
                    dve.tensor_copy(wq_y[:, at:at + SIZES[p] - s], diagonal(p, s))

            def block_of(out_t, offset, a0, na, c0, nc_):
                step = nc_
                if isinstance(offset, tuple):
                    offset, step = offset
                return dve.tensor_copy(view(out_t, offset, [(step, na), (1, nc_)]), wq[:, a0:a0 + na, c0:c0 + nc_])

            block_of(wq_cross, 0, e0, NE, f0, NF)
            block_of(wq_cross, NEF, d0, ND, e0, NE + NF)
            block_of(wq_cross, (CROSS, ND + NF), e0, NE, d0, ND)
            block_of(wq_cross, (CROSS + ND, ND + NF), e0, NE, f0, NF)
            block_of(wq_cross, CROSS + NE * (ND + NF), f0, NF, d0, ND)
            block_of(wq_cross, 2 * CROSS, f0, NF, d0, ND + NE)
            block_of(wq_cross, 2 * CROSS + NF * (ND + NE), e0, NE, d0, ND).then_inc(wq_ready, 1)

            settle(dve.memset(blk[:, :, :, :], 0.0))
            for q in range(QUADS):
                dve.memset(blk[32 * q:32 * q + 32, :, q, 0:1], 1.0)
            dve.memset(prod[:, :, ONE:ONE + 1], 1.0).then_inc(presets, 1)

            def products(c, first):
                for p in PARTS:
                    at, size = STARTS[p], SIZES[p]
                    dve.wait_ge(rows_in[p], 16 * size * (c + 1))
                    col = EMB_AT[p]
                    if not first:
                        dve.wait_ge(blk_copied, 2 * c)
                    dve.transpose(emb[:, :, col + size:col + size + WRAP[p]].rearrange("p g f -> p f g"),
                                  rows[:, at:at + WRAP[p], :])
                    dve.transpose(emb[:, :, col:col + size].rearrange("p g f -> p f g"),
                                  rows[:, at:at + size, :]).then_inc(rows_used[p], 1)
                    dve.wait_ge(rows_used[p], c + 1)
                    if p == PARTS[0] and not first:
                        dve.wait_ge(x_mm, NXB * c)
                    if p == D:
                        for q in range(QUADS):
                            dve.tensor_copy(*blk_views(p, q))
                    n, rows_at, gs = size, ROWS_AT[p], (EMB_COLS, GROUPS)
                    shifts = (n + 1) // 2
                    last = dve.tensor_tensor(view(prod, rows_at, [(PCOLS, GROUPS), (n, shifts), (1, n)]),
                                             view(emb, col, [gs, (0, shifts), (1, n)]),
                                             view(emb, col, [gs, (1, shifts), (1, n)]), ALU.mult)
                    if n % 2 == 0:
                        last = dve.tensor_tensor(prod[:, :, rows_at + n * shifts:rows_at + n * shifts + n // 2],
                                                 emb[:, :, col:col + n // 2], emb[:, :, col + n // 2:col + n], ALU.mult)
                    if p == F:
                        dve.tensor_tensor(view(prod, NY, [(PCOLS, GROUPS), (NF, NE), (1, NF)]),
                                          view(emb, EMB_AT[E], [gs, (1, NE), (0, NF)]),
                                          view(emb, EMB_AT[F], [gs, (0, NE), (1, NF)]), ALU.mult)
                        last = dve.tensor_copy(view(prod, NY + NEF, [(PCOLS, GROUPS), (NE, 2), (1, NE)]),
                                               view(emb, EMB_AT[E], [gs, (EMB_AT[F] - EMB_AT[E], 2), (1, NE)]))
                        last.then_inc(pairs_ready, 1)
                last.then_inc(prod_ready, 1)

            products(0, True)

            dve.wait_ge(cross_out, FIELDS)
            other, single = NY, NY + NEF
            wide = ND + NE

            def add_cross(which):
                for s in range(which, ND):
                    rows_at = shift_row(D, s)
                    dst = view(r, e0 * RCOLS + rows_at, [(1, ND - s), (RCOLS, NE + NF)])
                    src = single + ((s * RCOLS) if which == 0 else s * (NE + NF))
                    dve.tensor_tensor(dst, dst, view(r, src, [(RCOLS + NE + NF, ND - s), (1, NE + NF)]), ALU.add)
                part_row = ROWS_AT[F] - ROWS_AT[E]
                part_src = NE * RCOLS
                for s in range(which, NE):
                    rows_at, n = shift_row(E, s), NE - s
                    src = e0 * RCOLS + other + ((s * RCOLS) if which == 0 else s * wide)
                    dst = view(r, rows_at, [(part_row, 2), (1, n), (RCOLS, ND)])
                    dve.tensor_tensor(dst, dst, view(r, src, [(part_src, 2), (RCOLS + wide, n), (1, ND)]), ALU.add)
                    dst = view(r, f0 * RCOLS + rows_at, [(part_row - part_src, 2), (1, n), (RCOLS, NE)])
                    dve.tensor_tensor(dst, dst, view(r, src + ND, [(part_src, 2), (RCOLS + wide, n), (1, NE)]), ALU.add)
                dst = view(r, NY, [(NF, NE), (1, NF), (RCOLS, ND)])
                tail = NY + NE * wide
                if which == 0:
                    src = view(r, f0 * RCOLS + tail, [(ND, NE), (RCOLS, NF), (1, ND)])
                else:
                    src = view(r, e0 * RCOLS + tail, [(RCOLS, NE), (ND, NF), (1, ND)])
                return dve.tensor_tensor(dst, dst, src, ALU.add)

            settle(add_cross(0))
            add_cross(1).then_inc(cross_added, 1)

            with dve.Fori(1, CHUNKS) as c:
                products(c, False)

        @block.scalar
        def _(act):
            act.dma_start(wq_y[:, ONE:ONE + 1], b1).then_inc(b1_loaded, 16)
            act.dma_start(b2_col[:, :], b2).then_inc(b2_loaded, 16)
            act.wait_ge(b2_loaded, 16)
            act.activation(kb2[:, :], b2_col[:, :], ACT.Copy, scale=float(K)).then_inc(kb2_ready, 1)
            act.wait_ge(kb2_ready, 1)

            def turn_out(turns, first):
                for n, (what, c0, m) in enumerate(turns):
                    dst = {"uxy": None, "um": u_m, "vx": v_x, "vy": v_y}[what]
                    src = bank[TURN_BANKS[first + n]]
                    act.wait_ge(turned, first + n + 1)
                    if what == "uxy":
                        act.activation(u_y[:, :], src[0:NY, 0:HID], ACT.Copy)
                        ins = act.activation(u_x[:, :], src[0:NEF, HID:2 * HID], ACT.Copy)
                    else:
                        ins = act.activation(dst[:, c0:c0 + m, :].rearrange("p c h -> p (c h)"),
                                             src[0:dst.shape[0], 0:m * HID], ACT.Copy)
                    ins.then_inc(turned_out, 1)

            def blk_copy(c, first):
                for p in (E, F):
                    act.wait_ge(rows_used[p], c + 1)
                    if not first:
                        act.wait_ge(x_mm, NXB * c)
                    for q in range(QUADS):
                        ins = act.activation(*blk_views(p, q), ACT.Copy)
                    ins.then_inc(blk_copied, 1)

            def t_out(c, between=None):
                for n in range(NYB):
                    if between:
                        between(c - 1, n)
                    act.wait_ge(y_mm, NYB * c + n + 1)
                    act.activation(
                        view(t_y, n * YB, [(32, QUADS), (CHUNK, CY), (1, YB)], parts=NY),
                        view(ps_y[n % 2], 0, [(CY, QUADS), (1, CY), (QUADS * CY, YB)], parts=NY),
                        ACT.Copy).then_inc(y_out, 1)
                    if n % 2 == 1:
                        m = n // 2
                        act.wait_ge(x_mm, NXB * c + m + 1)
                        act.activation(
                            view(t_x, m * XB, [(32, QUADS), (CHUNK, CX), (1, XB)], parts=NX),
                            view(ps_x[m % 2], 0, [(CX, QUADS), (1, CX), (QUADS * CX, XB)], parts=NX),
                            ACT.Copy).then_inc(x_out, 1)

            def z_out(c, which, mm, done, bias):
                act.wait_ge(mm, c + 1)
                if bias is None:
                    act.activation(z[:, which, :], ps_z[which][:, 0:CHUNK], ACT.Copy).then_inc(done, 1)
                else:
                    act.activation(z[:, which, :], ps_z[which][:, 0:CHUNK], ACT.Identity, bias=bias).then_inc(done, 1)

            def relu(c, tiles, mm, done, dst, src, bias):
                for t in range(tiles):
                    act.wait_ge(mm, tiles * c + t + 1)
                    act.activation(dst[:, t, :], src[t][:, 0:CHUNK], ACT.Relu,
                                   bias=bias[:, t:t + 1]).then_inc(done, 1)

            def out_copy(c):
                act.wait_ge(out_mm, c + 1)
                act.activation(y[0:1, bass.ts(c, CHUNK)], ps_out[0:1, 0:CHUNK], ACT.Copy).then_inc(out_out, 1)

            def perceptron(c, step):
                if step == 0:
                    relu(c, U1T, h1_mm, h1_out, h1, ps_h1, bt1)
                    relu(c, U2T, h2_mm, h2_out, h2, ps_h2, bt2)
                if step == 2:
                    out_copy(c)

            for c in range(FIELDS):
                act.wait_ge(cross_mm, c + 1)
                act.activation(r[:, c, :], bank[c % CROSS_BANKS][:, 0:RCOLS], ACT.Copy).then_inc(cross_out, 1)
                if c == FIELDS - GATED - 1:
                    turn_out(TURN_U, 0)
                    act.wait_ge(presets, 1)
                    blk_copy(0, True)
            t_out(0)
            turn_out(TURN_V, len(TURN_U))
            blk_copy(1, False)
            act.wait_ge(mlp_loaded, MLP_LOADS)
            z_out(0, 1, z2_mm, z2_out, kb2[:, 0:1])
            z_out(0, 0, z1_mm, z1_out, None)
            with act.Fori(1, CHUNKS - 1) as c:
                t_out(c, perceptron)
                blk_copy(c + 1, False)
                z_out(c, 1, z2_mm, z2_out, kb2[:, 0:1])
                z_out(c, 0, z1_mm, z1_out, None)
            t_out(CHUNKS - 1, perceptron)
            z_out(CHUNKS - 1, 1, z2_mm, z2_out, kb2[:, 0:1])
            z_out(CHUNKS - 1, 0, z1_mm, z1_out, None)
            for step in range(NYB):
                perceptron(CHUNKS - 1, step)

        @block.tensor
        def _(pe):
            part_of = [p for p in range(3) for _ in range(SIZES[p])]
            pe.wait_ge(wq_ready, 1)
            pe.wait_ge(w2_loaded, 32)
            pe.wait_ge(b1_loaded, 16)
            busy = {4: (turned_out, 2), 6: (y_out, NYB), 8: (x_out, NXB), 10: (turned_out, 4)}

            def turn(turns, first):
                for n, (what, c0, m) in enumerate(turns):
                    at = first + n
                    if at in busy:
                        pe.wait_ge(*busy[at])
                    ps = bank[TURN_BANKS[at]]
                    for j in range(m):
                        if what == "uxy":
                            src = (wq_y[:, :], wq_cross[:, D, 0:NEF])[j]
                        elif what == "um":
                            src = wq_cross[:, D, NEF + j * MROWS:NEF + (j + 1) * MROWS]
                        else:
                            src = r[:, c0 + j, 0:NY] if what == "vy" else r[:, c0 + j, NY:NY + NEF]
                        ins = pe.transpose(ps[0:src.shape[1], j * HID:(j + 1) * HID], src, ident[:, :])
                    ins.then_inc(turned, 1)

            def t_matmuls(c, first, between=None):
                pe.wait_ge(prod_ready, c + 1)
                pe.wait_ge(blk_copied, 2 * (c + 1))
                for n in range(NYB):
                    if between:
                        between(c - 1, n)
                    if not first or n >= 2:
                        pe.wait_ge(y_out, NYB * c + n - 1)
                    for j in range(YB):
                        g = n * YB + j
                        ins = pe.matmul(ps_y[n % 2][0:NY, j * QUADS * CY:(j + 1) * QUADS * CY], prod[:, g, 0:NY],
                                        blk[:, g, :, :].rearrange("p q c -> p (q c)"), start=True, stop=True)
                    ins.then_inc(y_mm, 1)
                    if n % 2 == 1:
                        m = n // 2
                        if not first or m >= 2:
                            pe.wait_ge(x_out, NXB * c + m - 1)
                        for j in range(XB):
                            g = m * XB + j
                            ins = pe.matmul(ps_x[m % 2][0:NX, j * QUADS * CX:(j + 1) * QUADS * CX], prod[:, g, NY:],
                                            blk[:, g, :, 0:CX], start=True, stop=True)
                        ins.then_inc(x_mm, 1)

            def z2_matmuls(c, first):
                pe.wait_ge(y_out, NYB * (c + 1))
                if not first:
                    pe.wait_ge(z2_out, c)
                for j in range(FIELDS):
                    if first and j % 4 == 0:
                        pe.wait_ge(turned_out, len(TURN_U) + j // 4 + 1)
                    pe.matmul(ps_z[1][:, 0:CHUNK], v_y[:, j, :], t_y[:, 1 + j, :], start=(j == 0), stop=False)
                pe.wait_ge(x_out, NXB * (c + 1))
                if first:
                    pe.wait_ge(turned_out, len(TURN_U) + len(TURN_V))
                for j in range(ND):
                    ins = pe.matmul(ps_z[1][:, 0:CHUNK], v_x[:, j, :], t_x[0:NEF, 1 + j, :], start=False, stop=(j == ND - 1))
                ins.then_inc(z2_mm, 1)

            def z1_matmuls(c, first):
                if not first:
                    pe.wait_ge(out_out, c)
                pe.matmul(ps_z[0][:, 0:CHUNK], u_y[:, :], t_y[:, 0, :], start=True, stop=False)
                pe.matmul(ps_z[0][:, 0:CHUNK], u_x[:, :], t_x[0:NEF, 0, :], start=False, stop=False)
                pe.wait_ge(m_moved, 16 * ND * (c + 1))
                for j in range(2):
                    ins = pe.matmul(ps_z[0][:, 0:CHUNK], u_m[:, j, :], m_x[:, j, :], start=False, stop=(j == 1))
                ins.then_inc(z1_mm, 1)

            def mlp1(c):
                pe.wait_ge(z2_out, c + 1)
                for t in range(U1T):
                    ps = ps_h1[t][:, 0:CHUNK]
                    pe.matmul(ps, wt1d[:, t * 128:(t + 1) * 128], dense[:, bass.ts(c, CHUNK)], start=True, stop=False)
                    pe.matmul(ps, wt1[:, 1, t * 128:(t + 1) * 128], z[:, 1, :], start=False, stop=False)
                    if t == 0:
                        pe.wait_ge(z1_out, c + 1)
                    pe.matmul(ps, wt1[:, 0, t * 128:(t + 1) * 128], z[:, 0, :], start=False, stop=True).then_inc(h1_mm, 1)

            def mlp2(c):
                for t in range(U2T):
                    for k in range(U1T):
                        if t == 0:
                            pe.wait_ge(h1_out, U1T * c + k + 1)
                        ins = pe.matmul(ps_h2[t][:, 0:CHUNK], wt2[:, k, t * 128:(t + 1) * 128],
                                        h1[:, k, :], start=(k == 0), stop=(k == U1T - 1))
                    ins.then_inc(h2_mm, 1)

            def mlp3(c):
                for k in range(U2T):
                    pe.wait_ge(h2_out, U2T * c + k + 1)
                    ins = pe.matmul(ps_out[0:1, 0:CHUNK], wt3[:, k:k + 1], h2[:, k, :], start=(k == 0), stop=(k == U2T - 1))
                ins.then_inc(out_mm, 1)

            def perceptron(c, step):
                if step == 1:
                    mlp3(c)

            for c in range(FIELDS):
                if c == FIELDS - GATED:
                    pe.wait_ge(ident_ready, 2)
                    turn(TURN_U, 0)
                    pe.wait_ge(pairs_ready, 1)
                if c >= CROSS_BANKS:
                    pe.wait_ge(cross_out, c - CROSS_BANKS + 1)
                ps = bank[c % CROSS_BANKS]
                pe.matmul(ps[:, 0:NY], w2[:, c, :], wq_y[:, :], start=True, stop=True)
                pe.matmul(ps[:, NY:RCOLS], w2[:, c, :], wq_cross[:, part_of[c], :], start=True, stop=True).then_inc(cross_mm, 1)
            pe.wait_ge(cross_out, FIELDS)
            t_matmuls(0, True)
            pe.wait_ge(cross_added, 1)
            turn(TURN_V, len(TURN_U))
            pe.wait_ge(mlp_loaded, MLP_LOADS)
            z2_matmuls(0, True)
            z1_matmuls(0, True)
            with pe.Fori(1, CHUNKS) as c:
                pe.wait_ge(pairs_ready, c + 1)
                mlp1(c - 1)
                mlp2(c - 1)
                t_matmuls(c, False, perceptron)
                z2_matmuls(c, False)
                z1_matmuls(c, False)
            mlp1(CHUNKS - 1)
            mlp2(CHUNKS - 1)
            mlp3(CHUNKS - 1)


def kernel(**inputs):
    import numpy as np
    import concourse.bacc as bacc
    from concourse.bass_utils import run_bass_kernel_spmd

    nc = bacc.Bacc("TRN2", target_bir_lowering=False, num_devices=1)
    laid_out = {
        "dense_t": np.ascontiguousarray(np.transpose(inputs["dense_ctx"])),
        "ids": np.ascontiguousarray(inputs["ids"]),
        "w_top1": np.ascontiguousarray(inputs["W_top1"]),
        "b_top1": np.ascontiguousarray(np.transpose(np.reshape(inputs["b_top1"], (4, 128)))),
        "w_top2": np.ascontiguousarray(inputs["W_top2"]),
        "b_top2": np.ascontiguousarray(np.transpose(np.reshape(inputs["b_top2"], (2, 128)))),
        "w_top3": np.ascontiguousarray(np.transpose(np.reshape(inputs["W_top3"], (2, 128)))),
        "w1": np.ascontiguousarray(inputs["L0_rec_W1"]),
        "b1": np.ascontiguousarray(np.reshape(inputs["L0_rec_b1"], (128, 1))),
        "w2t": np.ascontiguousarray(np.transpose(inputs["L0_rec_W2"], (1, 2, 0))),
        "b2": np.ascontiguousarray(np.reshape(inputs["L0_rec_b2"], (128, 1))),
    }
    for f in range(FIELDS):
        laid_out[f"tbl_{f}"] = np.ascontiguousarray(inputs[f"tbl_{f}"])
    dram = {name: nc.dram_tensor(name, a.shape, mybir.dt.from_np(a.dtype), kind="ExternalInput").ap()
            for name, a in laid_out.items()}
    out = nc.dram_tensor("scores", (1, BATCH), mybir.dt.float32, kind="ExternalOutput").ap()
    tower_kernel(nc, dram["dense_t"], dram["ids"], [dram[f"tbl_{f}"] for f in range(FIELDS)],
                 dram["w_top1"], dram["b_top1"], dram["w_top2"], dram["b_top2"], dram["w_top3"],
                 dram["w1"], dram["b1"], dram["w2t"], dram["b2"], out)
    result = run_bass_kernel_spmd(nc, [laid_out], core_ids=[0])
    return np.reshape(result.results[0]["scores"], (BATCH, 1))
```

```python
import concourse.bass as bass
from concourse import mybir
from concourse.alu_op_type import AluOpType as ALU
from contextlib import ExitStack

FIELDS, K, BATCH, HID = 26, 32, 512, 128
CHUNK = 128
CHUNKS = BATCH // CHUNK
QUADS = 4
GROUPS = CHUNK // QUADS
STARTS, SIZES = (0, 10, 18), (10, 8, 8)
D, E, F = 0, 1, 2
ND, NE, NF = SIZES
LATE = 2
LOOKED_UP = (STARTS[F] + NF - 1, STARTS[D] + ND - 1)
LOOKUPS = len(LOOKED_UP)
VROWS, VTILES = 125, 8
SPLIT = 3
BATCHES = ((E, 0, NE, 0), (F, 0, NF - 1, 1), (D, 0, ND - 1 - LATE, 0), (D, ND - 1 - LATE, ND - 1, 1))
D_EARLY, D_LATE = 2, 3
TRI = [n * (n + 1) // 2 for n in SIZES]
ROWS_AT = (0, TRI[0], TRI[0] + TRI[1])
ONE = sum(TRI)
NY = ONE + 1
NEF = NE * NF
NX = NEF + NE + NF
CY = FIELDS + 1
CX = ND + 1
PCOLS = NY + NX
CROSS = NEF + ND * (NE + NF)
MROWS = CROSS // 2
DEEP = ND // 2
RCOLS = NY + CROSS
WRAP = tuple(n // 2 - 1 for n in SIZES)
EMB_AT = (0, ND + WRAP[0], ND + NE + WRAP[0] + WRAP[1])
EMB_COLS = FIELDS + sum(WRAP)
YB, XB = 4, 8
U1, U2 = 512, 256


def shift_row(part, s):
    n = SIZES[part]
    return ROWS_AT[part] + (s * n if s <= n // 2 else (n - s) * n + s)


def tower_kernel(nc, dense_t, ids, ids_rows, first_rows, tables, w_top1, b_top1, w_top2, b_top2, w_top3,
                 w1, b1, w2t, b2, out):
    f32, i32, bf16 = mybir.dt.float32, mybir.dt.int32, mybir.dt.bfloat16
    ACT = mybir.ActivationFunctionType
    assert NY == 128 and NEF == 64 and ND % 2 == 0 and NE == NF and (MROWS - NEF) % (NE + NF) == 0
    assert all(tables[f].shape[0] == VROWS * VTILES for f in LOOKED_UP)

    with ExitStack() as ctx:
        def sb(name, shape, dt=f32):
            return ctx.enter_context(nc.sbuf_tensor(name, shape, dt))

        def sem(name):
            return ctx.enter_context(nc.semaphore(name))

        def view(t, offset, dims, at=0, parts=128):
            row = 1
            for n in t.shape[1:]:
                row *= n
            return bass.AP(t, at * row + offset, [[row, parts]] + [list(d) for d in dims])

        ids_all = sb("ids_all", [128, CHUNKS, FIELDS], i32)
        rows = sb("rows", [128, FIELDS, K])
        emb = sb("emb", [128, GROUPS, EMB_COLS])
        blk = sb("blk", [128, GROUPS, QUADS, CY])
        prod = sb("prod", [128, GROUPS, PCOLS])
        t_y = sb("t_y", [NY, CY, CHUNK])
        t_x = sb("t_x", [128, 1 + DEEP, CHUNK])
        t_f = sb("t_f", [128, ND, CHUNK])
        ids_p = sb("ids_p", [VROWS, LOOKUPS * BATCH], i32)
        first_row = sb("first_row", [VROWS, 1])
        ids_off = sb("ids_off", [VROWS, LOOKUPS * BATCH], bf16)
        one_hot = sb("one_hot", [VROWS, VTILES, LOOKUPS * BATCH], bf16)
        table = sb("table", [VROWS, LOOKUPS, VTILES * K])
        table_rest = sb("table_rest", [VROWS, LOOKUPS, VTILES * K])
        table_split = sb("table_split", [VROWS, VTILES, LOOKUPS, SPLIT * K], bf16)
        rows_split = sb("rows_split", [SPLIT * K, LOOKUPS * CHUNKS, QUADS, GROUPS])
        sum_split = sb("sum_split", [SPLIT * K, (2 * QUADS - 1) * K])
        looked_up = sb("looked_up", [128, LOOKUPS * CHUNKS, GROUPS])
        w1_raw = sb("w1_raw", [128, FIELDS, FIELDS])
        wq = sb("wq", [128, FIELDS, FIELDS])
        w2 = sb("w2", [128, FIELDS, HID])
        wq_y = sb("wq_y", [128, NY])
        wq_m = sb("wq_m", [128, 2, MROWS])
        wq_cross = sb("wq_cross", [128, 3, CROSS])
        r = sb("r", [128, FIELDS, RCOLS])
        s_x = sb("s_x", [128, ND, NEF])
        v_y = sb("v_y", [NY, FIELDS, HID])
        v_x = sb("v_x", [2 * NEF, DEEP, HID])
        u_y = sb("u_y", [NY, HID])
        u_m = sb("u_m", [MROWS, 2, HID])
        m_x = sb("m_x", [MROWS, 2, CHUNK])
        ident = sb("ident", [128, 128])
        b2_col = sb("b2_col", [128, 1])
        kb2 = sb("kb2", [128, 1])
        z = sb("z", [128, 2, CHUNK])
        dense = sb("dense", [16, BATCH])
        wt1 = sb("wt1", [128, 2, U1])
        wt1d = sb("wt1d", [16, U1])
        bt1 = sb("bt1", [128, U1 // 128])
        wt2 = sb("wt2", [128, U1 // 128, U2])
        bt2 = sb("bt2", [128, U2 // 128])
        wt3 = sb("wt3", [128, U2 // 128])
        h1 = sb("h1", [128, U1 // 128, CHUNK])
        h2 = sb("h2", [128, U2 // 128, CHUNK])
        y = sb("y", [1, BATCH])

        bank = [ctx.enter_context(nc.psum_tensor(f"bank{n}", [128, 512], f32)) for n in range(8)]
        ps_y, ps_x = bank[0:2], bank[2:4]
        ps_z = bank[4:6]
        ps_h1 = (bank[6], bank[7], bank[4], bank[5])
        ps_h2, ps_out = (bank[6], bank[7]), bank[4]

        ids_loaded, w1_loaded, w2_loaded, b1_loaded = sem("ids_loaded"), sem("w1_loaded"), sem("w2_loaded"), sem("b1_loaded")
        mlp_loaded, b2_loaded = sem("mlp_loaded"), sem("b2_loaded")
        rows_in = [sem(f"rows_in{p}") for p in range(len(BATCHES))]
        rows_used = [sem(f"rows_used{p}") for p in range(len(BATCHES))]
        presets = sem("presets")
        table_loaded, ids_rows_loaded = sem("table_loaded"), sem("ids_rows_loaded")
        table_high = sem("table_high")
        table_split_done = sem("table_split_done")
        one_hot_ready = sem("one_hot_ready")
        sum_split_ready = sem("sum_split_ready")
        lookup_mm, lookup_out = sem("lookup_mm"), sem("lookup_out")
        summed, sum_out = sem("summed"), sem("sum_out")
        ident_ready = sem("ident_ready")
        dve_done = sem("dve_done")
        wq_ready, wq_m_ready = sem("wq_ready"), sem("wq_m_ready")
        cross_mm, cross_out = sem("cross_mm"), sem("cross_out")
        cross_added = sem("cross_added")
        turned, turned_out = sem("turned"), sem("turned_out")
        kb2_ready = sem("kb2_ready")
        blk_copied = sem("blk_copied")
        prod_ready = sem("prod_ready")
        y_mm, x_mm = sem("y_mm"), sem("x_mm")
        y_out, x_out = sem("y_out"), sem("x_out")
        z2_mm, z1_mm, z2_out, z1_out = sem("z2_mm"), sem("z1_mm"), sem("z2_out"), sem("z1_out")
        m_moved = sem("m_moved")
        h1_mm, h1_out, h2_mm, h2_out = sem("h1_mm"), sem("h1_out"), sem("h2_mm"), sem("h2_out")
        out_mm, out_out, stored = sem("out_mm"), sem("out_out"), sem("stored")

        NYB, NXB = GROUPS // YB, GROUPS // XB
        TURN_U = [("uy", 0, 1), ("um", 0, 2)]
        TURN_X = [("vx", n, min(4, DEEP - n)) for n in range(0, DEEP, 4)]
        TURN_V = TURN_X + [("vy", n, min(4, FIELDS - n)) for n in range(0, FIELDS, 4)]
        U1T, U2T = U1 // 128, U2 // 128
        D0 = (MROWS - NEF) // (NE + NF)
        M_D = ((0, NEF, 0, D0), (1, 0, D0, ND - D0))
        M_LOADS = (1 + len(M_D)) * 16
        MLP_LOADS = 7 * 16
        CROSS_BANKS = 6
        CROSS_FIRST = (-FIELDS) % CROSS_BANKS
        TURN_BANKS = (6, 7) + (5, 4, 6, 7, 0, 1, 2, 3, 4)
        SUM_AT, TURN_AT, HALFWAY = 5, 9, 16

        block = ctx.enter_context(nc.Block())

        @block.sync
        def _(sp):
            sp.dma_start(ids_all[:, :, :], ids.rearrange("(c p) f -> p c f", p=CHUNK)).then_inc(ids_loaded, 16)
            for n, f in enumerate(LOOKED_UP):
                sp.dma_start(table[:, n, :], tables[f].rearrange("(p t) k -> p (t k)", t=VTILES)).then_inc(table_loaded, 16)
            sp.dma_start(w1_raw[:, :, :], w1).then_inc(w1_loaded, 16)
            half = FIELDS // 2
            sp.dma_start(w2[:, 0:half, :], w2t[:, 0:half, :]).then_inc(w2_loaded, 16)
            sp.dma_start(w2[:, half:, :], w2t[:, half:, :]).then_inc(w2_loaded, 16)
            sp.dma_start(wq_y[:, ONE:ONE + 1], b1).then_inc(b1_loaded, 16)
            sp.dma_start(b2_col[:, :], b2).then_inc(b2_loaded, 16)
            sp.dma_start(wt1[:, :, :], w_top1[0:2 * HID, :].rearrange("(t p) n -> p t n", p=128)).then_inc(mlp_loaded, 16)
            sp.dma_start(wt1d[:, :], w_top1[2 * HID:, :]).then_inc(mlp_loaded, 16)
            sp.dma_start(dense[:, :], dense_t).then_inc(mlp_loaded, 16)
            sp.dma_start(wt2[:, :, :], w_top2.rearrange("(t p) n -> p t n", p=128)).then_inc(mlp_loaded, 16)
            sp.dma_start(bt1[:, :], b_top1).then_inc(mlp_loaded, 16)
            sp.dma_start(bt2[:, :], b_top2).then_inc(mlp_loaded, 16)
            sp.dma_start(wt3[:, :], w_top3).then_inc(mlp_loaded, 16)
            def move_m(c, first):
                sp.wait_ge(x_out, NXB * (c + 1))
                if not first:
                    sp.wait_ge(z1_mm, c)
                sp.dma_start(m_x[0:NEF, 0, :], t_x[NEF:2 * NEF, 0, :]).then_inc(m_moved, 16)
                for n, rows_at, j0, nj in M_D:
                    sp.dma_start(m_x[rows_at:rows_at + nj * (NE + NF), n, :], t_f[NEF:NX, j0:j0 + nj, :]).then_inc(m_moved, 16)

            move_m(0, True)
            with sp.Fori(1, CHUNKS) as c:
                move_m(c, False)
            sp.wait_ge(out_out, CHUNKS)
            sp.dma_start(out, y[:, :]).then_inc(stored, 16)
            sp.wait_ge(stored, 16)

        @block.gpsimd
        def _(pool):
            pool.memset(ident[:, :], 0.0).then_inc(ident_ready, 1)
            pool.wait_ge(ident_ready, 1)
            pool.affine_select(out=ident[:, :], in_=ident[:, :], compare_op=ALU.not_equal, fill=1.0, base=0,
                               pattern=[[-1, 128]], channel_multiplier=1).then_inc(ident_ready, 1)
            pool.wait_ge(ids_loaded, 16)

            for c in range(CHUNKS):
                for n, (p, lo, hi, _) in enumerate(BATCHES):
                    if c > 0:
                        pool.wait_ge(rows_used[n], c)
                    for f in range(STARTS[p] + lo, STARTS[p] + hi):
                        pool.indirect_dma_start(
                            rows[:, f, :], None, tables[f],
                            bass.IndirectOffsetOnAxis(ap=ids_all[:, c, f:f + 1], axis=0)).then_inc(rows_in[n], 16)

        def diagonal(part, s):
            return view(wq, STARTS[part] * (FIELDS + 1) + s, [(FIELDS + 1, SIZES[part] - s)])

        def blk_views(batch, q):
            p, lo, hi, extra = BATCHES[batch]
            hi += extra
            here = slice(32 * q, 32 * q + 32)
            return (blk[here, :, q, 1 + STARTS[p] + lo:1 + STARTS[p] + hi],
                    emb[here, :, EMB_AT[p] + lo:EMB_AT[p] + hi])

        @block.vector
        def _(dve):
            steps = [0]

            def settle(instruction):
                steps[0] += 1
                instruction.then_inc(dve_done, 1)
                dve.wait_ge(dve_done, steps[0])

            dve.memset(sum_split[:, 0:(QUADS - 1) * K], 0.0)
            dve.memset(sum_split[:, QUADS * K:], 0.0).then_inc(sum_split_ready, 1)
            dve.wait_ge(ids_rows_loaded, 32)
            settle(dve.tensor_scalar(ids_off[:, :], ids_p[:, :], first_row[:, 0:1], None, ALU.subtract))
            dve.wait_ge(table_high, 1)
            high, middle, low = [table_split[:, :, :, m * K:(m + 1) * K].rearrange("p t f k -> p f t k") for m in range(SPLIT)]
            whole = table[:, :, :].rearrange("p f (t k) -> p f t k", k=K)
            rest = table_rest[:, :, :].rearrange("p f (t k) -> p f t k", k=K)
            settle(dve.tensor_tensor(rest, whole, high, ALU.subtract))
            settle(dve.tensor_copy(middle, rest))
            dve.tensor_tensor(low, rest, middle, ALU.subtract).then_inc(table_split_done, 1)
            for t in range(VTILES):
                dve.tensor_scalar(one_hot[:, t, :], ids_off[:, :], float(t), None, ALU.is_equal).then_inc(one_hot_ready, 1)

            dve.wait_ge(w1_loaded, 16)
            settle(dve.tensor_tensor(wq[:, :, :], w1_raw[:, :, :], w1_raw[:, :, :].rearrange("p a b -> p b a"), ALU.add))
            settle(dve.tensor_copy(view(wq, 0, [(FIELDS + 1, FIELDS)]), view(w1_raw, 0, [(FIELDS + 1, FIELDS)])))
            d0, e0, f0 = STARTS
            for p in range(3):
                for s in range(SIZES[p]):
                    at = shift_row(p, s)
                    dve.tensor_copy(wq_y[:, at:at + SIZES[p] - s], diagonal(p, s))

            def block_of(out_t, offset, a0, na, c0, nc_):
                step = nc_
                if isinstance(offset, tuple):
                    offset, step = offset
                return dve.tensor_copy(view(out_t, offset, [(step, na), (1, nc_)]), wq[:, a0:a0 + na, c0:c0 + nc_])

            block_of(wq_cross, 0, e0, NE, f0, NF)
            block_of(wq_cross, NEF, d0, ND, e0, NE + NF)
            block_of(wq_cross, (CROSS, ND + NF), e0, NE, d0, ND)
            block_of(wq_cross, (CROSS + ND, ND + NF), e0, NE, f0, NF)
            block_of(wq_cross, CROSS + NE * (ND + NF), f0, NF, d0, ND)
            block_of(wq_cross, 2 * CROSS, f0, NF, d0, ND + NE)
            block_of(wq_cross, 2 * CROSS + NF * (ND + NE), e0, NE, d0, ND).then_inc(wq_ready, 1)

            block_of(wq_m, 0, e0, NE, f0, NF)
            for n, rows_at, j0, nj in M_D:
                ins = block_of(wq_m, n * MROWS + rows_at, e0, NE + NF, d0 + j0, nj)
            ins.then_inc(wq_m_ready, 1)

            settle(dve.memset(blk[:, :, :, :], 0.0))
            for q in range(QUADS):
                dve.memset(blk[32 * q:32 * q + 32, :, q, 0:1], 1.0)
            dve.memset(prod[:, :, ONE:ONE + 1], 1.0).then_inc(presets, 1)

            def turn_rows(batch, c):
                p, lo, hi, extra = BATCHES[batch]
                at, col, wrap = STARTS[p], EMB_AT[p], min(hi, WRAP[p]) if lo == 0 else 0
                if extra:
                    n = LOOKED_UP.index(at + hi)
                    dve.wait_ge(sum_out, 1)
                    dve.tensor_copy(emb[:, :, col + hi], looked_up[:, n * CHUNKS + c, :])
                dve.wait_ge(rows_in[batch], 16 * (hi - lo) * (c + 1))
                if wrap:
                    dve.transpose(emb[:, :, col + SIZES[p]:col + SIZES[p] + wrap].rearrange("p g f -> p f g"),
                                  rows[:, at:at + wrap, :])
                dve.transpose(emb[:, :, col + lo:col + hi].rearrange("p g f -> p f g"),
                              rows[:, at + lo:at + hi, :]).then_inc(rows_used[batch], 1)
                dve.wait_ge(rows_used[batch], c + 1)

            def pairs(p, g0, g1):
                n, rows_at, gs, ng = SIZES[p], ROWS_AT[p], (EMB_COLS, g1 - g0), g1 - g0
                shifts = (n + 1) // 2
                at, col = g0 * PCOLS + rows_at, g0 * EMB_COLS + EMB_AT[p]
                ins = dve.tensor_tensor(view(prod, at, [(PCOLS, ng), (n, shifts), (1, n)]),
                                        view(emb, col, [gs, (0, shifts), (1, n)]),
                                        view(emb, col, [gs, (1, shifts), (1, n)]), ALU.mult)
                if n % 2 == 0:
                    ins = dve.tensor_tensor(view(prod, at + n * shifts, [(PCOLS, ng), (1, n // 2)]),
                                            view(emb, col, [gs, (1, n // 2)]),
                                            view(emb, col + n // 2, [gs, (1, n // 2)]), ALU.mult)
                return ins

            def products(c, first):
                if not first:
                    dve.wait_ge(blk_copied, 2 * c)
                turn_rows(0, c)
                if not first:
                    dve.wait_ge(y_mm, NYB * c)
                pairs(E, 0, GROUPS)
                turn_rows(1, c)
                pairs(F, 0, GROUPS)
                gs = (EMB_COLS, GROUPS)
                dve.tensor_tensor(view(prod, NY, [(PCOLS, GROUPS), (NF, NE), (1, NF)]),
                                  view(emb, EMB_AT[E], [gs, (1, NE), (0, NF)]),
                                  view(emb, EMB_AT[F], [gs, (0, NE), (1, NF)]), ALU.mult)
                dve.tensor_copy(view(prod, NY + NEF, [(PCOLS, GROUPS), (NE, 2), (1, NE)]),
                                view(emb, EMB_AT[E], [gs, (EMB_AT[F] - EMB_AT[E], 2), (1, NE)]))
                for batch in (D_EARLY, D_LATE):
                    turn_rows(batch, c)
                    for q in range(QUADS):
                        dve.tensor_copy(*blk_views(batch, q))
                pairs(D, 0, XB).then_inc(prod_ready, 1)
                pairs(D, XB, GROUPS).then_inc(prod_ready, 1)

            products(0, True)

            dve.wait_ge(cross_out, FIELDS)
            other, single = NY, NY + NEF
            wide = ND + NE

            def add_cross(which):
                for s in range(which, ND):
                    rows_at = shift_row(D, s)
                    dst = view(r, e0 * RCOLS + rows_at, [(1, ND - s), (RCOLS, NE + NF)])
                    src = single + ((s * RCOLS) if which == 0 else s * (NE + NF))
                    dve.tensor_tensor(dst, dst, view(r, src, [(RCOLS + NE + NF, ND - s), (1, NE + NF)]), ALU.add)
                part_row = ROWS_AT[F] - ROWS_AT[E]
                part_src = NE * RCOLS
                for s in range(which, NE):
                    rows_at, n = shift_row(E, s), NE - s
                    src = e0 * RCOLS + other + ((s * RCOLS) if which == 0 else s * wide)
                    dst = view(r, rows_at, [(part_row, 2), (1, n), (RCOLS, ND)])
                    dve.tensor_tensor(dst, dst, view(r, src, [(part_src, 2), (RCOLS + wide, n), (1, ND)]), ALU.add)
                    dst = view(r, f0 * RCOLS + rows_at, [(part_row - part_src, 2), (1, n), (RCOLS, NE)])
                    dve.tensor_tensor(dst, dst, view(r, src + ND, [(part_src, 2), (RCOLS + wide, n), (1, NE)]), ALU.add)
                dst = view(r, NY, [(NF, NE), (1, NF), (RCOLS, ND)])
                tail = NY + NE * wide
                if which == 0:
                    src = view(r, f0 * RCOLS + tail, [(ND, NE), (RCOLS, NF), (1, ND)])
                else:
                    src = view(r, e0 * RCOLS + tail, [(RCOLS, NE), (ND, NF), (1, ND)])
                sum_t = dst if which == 0 else view(s_x, 0, [(NF, NE), (1, NF), (NEF, ND)])
                return dve.tensor_tensor(sum_t, dst, src, ALU.add)

            settle(add_cross(0))
            add_cross(1).then_inc(cross_added, 1)

            with dve.Fori(1, CHUNKS) as c:
                products(c, False)

        @block.scalar
        def _(act):
            act.dma_start(ids_p[:, :], ids_rows.partition_broadcast(VROWS)).then_inc(ids_rows_loaded, 16)
            act.dma_start(first_row[:, :], first_rows).then_inc(ids_rows_loaded, 16)
            act.wait_ge(ident_ready, 2)
            for m in range(SPLIT):
                here = slice(m * K, (m + 1) * K)
                ins = act.activation(sum_split[here, (QUADS - 1) * K:QUADS * K], ident[here, here], ACT.Copy)
            ins.then_inc(sum_split_ready, 1)
            act.wait_ge(table_loaded, 16 * LOOKUPS)
            act.activation(table_split[:, :, :, 0:K].rearrange("p t f k -> p f t k"),
                           table[:, :, :].rearrange("p f (t k) -> p f t k", k=K), ACT.Copy).then_inc(table_high, 1)

            def turn_out(turns, first):
                for n, (what, c0, m) in enumerate(turns):
                    dst = {"uy": None, "um": u_m, "vx": v_x, "vy": v_y}[what]
                    src = bank[TURN_BANKS[first + n]]
                    act.wait_ge(turned, first + n + 1)
                    if what == "uy":
                        ins = act.activation(u_y[:, :], src[0:NY, 0:HID], ACT.Copy)
                    else:
                        ins = act.activation(dst[:, c0:c0 + m, :].rearrange("p c h -> p (c h)"),
                                             src[0:dst.shape[0], 0:m * HID], ACT.Copy)
                    ins.then_inc(turned_out, 1)

            def blk_copy(c, first):
                for batch in (0, 1):
                    act.wait_ge(rows_used[batch], c + 1)
                    if not first:
                        act.wait_ge(y_mm, NYB * c)
                    for q in range(QUADS):
                        ins = act.activation(*blk_views(batch, q), ACT.Copy)
                    ins.then_inc(blk_copied, 1)

            def relu(c, tiles, mm, done, dst, src, bias):
                for t in range(tiles):
                    act.wait_ge(mm, tiles * c + t + 1)
                    act.activation(dst[:, t, :], src[t][:, 0:CHUNK], ACT.Relu,
                                   bias=bias[:, t:t + 1]).then_inc(done, 1)

            def perceptron(c):
                relu(c, U1T, h1_mm, h1_out, h1, ps_h1, bt1)
                relu(c, U2T, h2_mm, h2_out, h2, ps_h2, bt2)

            def score_out(c):
                act.wait_ge(out_mm, c + 1)
                act.activation(y[0:1, bass.ts(c, CHUNK)], ps_out[0:1, 0:CHUNK], ACT.Copy).then_inc(out_out, 1)

            def t_out(c, first):
                for n in range(NYB):
                    if n == 2 and not first:
                        score_out(c - 1)
                    act.wait_ge(y_mm, NYB * c + n + 1)
                    act.activation(
                        view(t_y, n * YB, [(32, QUADS), (CHUNK, CY), (1, YB)], parts=NY),
                        view(ps_y[n % 2], 0, [(CY, QUADS), (1, CY), (QUADS * CY, YB)], parts=NY),
                        ACT.Copy).then_inc(y_out, 1)
                    if n < NXB:
                        m = n
                        act.wait_ge(x_mm, NXB * c + m + 1)
                        for dst, first_slot, first_col, step, cols, at, src_at, parts in (
                                (t_x, 0, 0, 2, 1 + DEEP, NEF, 0, NEF),
                                (t_x, 1, 1, 2, DEEP, 0, 0, NEF),
                                (t_f, 0, 1, 1, ND, NEF, NEF, NE + NF)):
                            ins = act.activation(
                                view(dst, first_slot * CHUNK + m * XB, [(32, QUADS), (CHUNK, cols), (1, XB)], at, parts),
                                view(ps_x[m % 2], first_col, [(CX, QUADS), (step, cols), (QUADS * CX, XB)], src_at, parts),
                                ACT.Copy)
                        ins.then_inc(x_out, 1)

            def z_out(c, which, mm, done, bias):
                act.wait_ge(mm, c + 1)
                if bias is None:
                    act.activation(z[:, which, :], ps_z[which][:, 0:CHUNK], ACT.Copy).then_inc(done, 1)
                else:
                    act.activation(z[:, which, :], ps_z[which][:, 0:CHUNK], ACT.Identity, bias=bias).then_inc(done, 1)

            act.wait_ge(b2_loaded, 16)
            act.activation(kb2[:, :], b2_col[:, :], ACT.Copy, scale=float(K)).then_inc(kb2_ready, 1)
            act.wait_ge(kb2_ready, 1)
            act.wait_ge(lookup_mm, 1)
            for n in range(LOOKUPS):
                act.activation(rows_split[:, n * CHUNKS:(n + 1) * CHUNKS, :, :].rearrange("p c q g -> p (c q g)"),
                               bank[6 + n][0:SPLIT * K, 0:BATCH], ACT.Copy).then_inc(lookup_out, 1)
            for c in range(FIELDS):
                act.wait_ge(cross_mm, c + 1)
                act.activation(r[:, c, :], bank[(c + CROSS_FIRST) % CROSS_BANKS][:, 0:RCOLS], ACT.Copy).then_inc(cross_out, 1)
                if c == TURN_AT - 1:
                    turn_out(TURN_U, 0)
                if c == SUM_AT - 1:
                    act.wait_ge(summed, 1)
                    act.activation(looked_up[:, :, :].rearrange("p c g -> p (c g)"), bank[6][:, 0:LOOKUPS * CHUNKS * GROUPS],
                                   ACT.Copy).then_inc(sum_out, 1)
                if c == HALFWAY - 1:
                    act.wait_ge(presets, 1)
                    blk_copy(0, True)
            t_out(0, True)
            turn_out(TURN_V, len(TURN_U))
            blk_copy(1, False)
            act.wait_ge(mlp_loaded, MLP_LOADS)
            z_out(0, 0, z1_mm, z1_out, None)
            z_out(0, 1, z2_mm, z2_out, kb2[:, 0:1])
            with act.Fori(1, CHUNKS - 1) as c:
                perceptron(c - 1)
                t_out(c, False)
                blk_copy(c + 1, False)
                z_out(c, 0, z1_mm, z1_out, None)
                z_out(c, 1, z2_mm, z2_out, kb2[:, 0:1])
            perceptron(CHUNKS - 2)
            t_out(CHUNKS - 1, False)
            z_out(CHUNKS - 1, 0, z1_mm, z1_out, None)
            z_out(CHUNKS - 1, 1, z2_mm, z2_out, kb2[:, 0:1])
            perceptron(CHUNKS - 1)
            score_out(CHUNKS - 1)

        @block.tensor
        def _(pe):
            part_of = [p for p in range(3) for _ in range(SIZES[p])]
            pe.wait_ge(table_split_done, 1)
            for t in range(VTILES):
                pe.wait_ge(one_hot_ready, t + 1)
                for n in range(LOOKUPS):
                    ins = pe.matmul(bank[6 + n][0:SPLIT * K, 0:BATCH], table_split[:, t, n, :],
                                    one_hot[:, t, n * BATCH:(n + 1) * BATCH], start=(t == 0), stop=(t == VTILES - 1))
            ins.then_inc(lookup_mm, 1)
            pe.wait_ge(wq_ready, 1)
            pe.wait_ge(w2_loaded, 32)
            pe.wait_ge(b1_loaded, 16)
            busy = {0: (sum_out, 1), 4: (turned_out, 2), 6: (y_out, NYB), 8: (x_out, NXB), 10: (turned_out, 4)}

            def turn(turns, first):
                for n, (what, c0, m) in enumerate(turns):
                    at = first + n
                    if at in busy:
                        pe.wait_ge(*busy[at])
                    ps = bank[TURN_BANKS[at]]
                    for j in range(m):
                        if what == "uy":
                            src = wq_y[:, :]
                        elif what == "um":
                            src = wq_m[:, j, :]
                        elif what == "vy":
                            src = r[:, c0 + j, 0:NY]
                        else:
                            src = view(s_x, 2 * (c0 + j) * NEF, [(1, 2 * NEF)])
                        ins = pe.transpose(ps[0:{"um": MROWS}.get(what, 128), j * HID:(j + 1) * HID], src, ident[:, :])
                    ins.then_inc(turned, 1)

            def mlp3(c):
                for k in range(U2T):
                    pe.wait_ge(h2_out, U2T * c + k + 1)
                    ins = pe.matmul(ps_out[0:1, 0:CHUNK], wt3[:, k:k + 1], h2[:, k, :], start=(k == 0), stop=(k == U2T - 1))
                ins.then_inc(out_mm, 1)

            def dense_matmuls(c, tiles):
                for t in tiles:
                    pe.matmul(ps_h1[t][:, 0:CHUNK], wt1d[:, t * 128:(t + 1) * 128], dense[:, bass.ts(c, CHUNK)],
                              start=True, stop=False)

            def t_matmuls(c, first):
                pe.wait_ge(prod_ready, 2 * c + 1)
                pe.wait_ge(blk_copied, 2 * (c + 1))
                for n in range(NYB):
                    if n == 1:
                        pe.wait_ge(prod_ready, 2 * c + 2)
                        if not first:
                            mlp3(c - 1)
                            dense_matmuls(c, range(2))
                    if not first or n >= 2:
                        pe.wait_ge(y_out, NYB * c + n - 1)
                    for j in range(YB):
                        g = n * YB + j
                        ins = pe.matmul(ps_y[n % 2][0:NY, j * QUADS * CY:(j + 1) * QUADS * CY], prod[:, g, 0:NY],
                                        blk[:, g, :, :].rearrange("p q c -> p (q c)"), start=True, stop=True)
                    ins.then_inc(y_mm, 1)
                    if n < NXB:
                        m = n
                        if not first or m >= 2:
                            pe.wait_ge(x_out, NXB * c + m - 1)
                        for j in range(XB):
                            g = m * XB + j
                            ins = pe.matmul(ps_x[m % 2][0:NX, j * QUADS * CX:(j + 1) * QUADS * CX], prod[:, g, NY:],
                                            blk[:, g, :, 0:CX], start=True, stop=True)
                        ins.then_inc(x_mm, 1)

            def z_matmuls(c, first):
                pe.wait_ge(x_out, NXB * (c + 1))
                if first:
                    pe.wait_ge(turned_out, len(TURN_U) + len(TURN_X))
                else:
                    pe.wait_ge(z2_out, c)
                for j in range(DEEP):
                    pe.matmul(ps_z[1][:, 0:CHUNK], v_x[:, j, :], t_x[:, 1 + j, :], start=(j == 0), stop=False)
                pe.wait_ge(y_out, NYB * (c + 1))

                def z2_from_y(columns):
                    for j in columns:
                        if first and j % 4 == 0:
                            pe.wait_ge(turned_out, len(TURN_U) + len(TURN_X) + j // 4 + 1)
                        ins = pe.matmul(ps_z[1][:, 0:CHUNK], v_y[:, j, :], t_y[:, 1 + j, :],
                                        start=False, stop=(j == FIELDS - 1))
                    return ins

                late = FIELDS - 4
                z2_from_y(range(late))
                if first:
                    pe.wait_ge(turned_out, len(TURN_U) + len(TURN_V))
                else:
                    pe.wait_ge(out_out, c)
                pe.matmul(ps_z[0][:, 0:CHUNK], u_y[:, :], t_y[:, 0, :], start=True, stop=False)
                pe.wait_ge(m_moved, M_LOADS * (c + 1))
                for j in range(2):
                    ins = pe.matmul(ps_z[0][:, 0:CHUNK], u_m[:, j, :], m_x[:, j, :], start=False, stop=(j == 1))
                ins.then_inc(z1_mm, 1)
                z2_from_y(range(late, FIELDS)).then_inc(z2_mm, 1)

            def mlp1(c):
                pe.wait_ge(z1_out, c + 1)
                for tiles in (range(3), range(3, U1T)):
                    dense_matmuls(c, tiles if tiles[0] > 0 else tiles[2:])
                    for t in tiles:
                        pe.matmul(ps_h1[t][:, 0:CHUNK], wt1[:, 0, t * 128:(t + 1) * 128], z[:, 0, :], start=False, stop=False)
                    if tiles[0] == 0:
                        pe.wait_ge(z2_out, c + 1)
                    for t in tiles:
                        pe.matmul(ps_h1[t][:, 0:CHUNK], wt1[:, 1, t * 128:(t + 1) * 128], z[:, 1, :],
                                  start=False, stop=True).then_inc(h1_mm, 1)

            def mlp2(c):
                for t in range(U2T):
                    for k in range(U1T):
                        if t == 0:
                            pe.wait_ge(h1_out, U1T * c + k + 1)
                        ins = pe.matmul(ps_h2[t][:, 0:CHUNK], wt2[:, k, t * 128:(t + 1) * 128],
                                        h1[:, k, :], start=(k == 0), stop=(k == U1T - 1))
                    ins.then_inc(h2_mm, 1)

            for c in range(FIELDS):
                if c == TURN_AT:
                    pe.wait_ge(ident_ready, 2)
                    pe.wait_ge(wq_m_ready, 1)
                    turn(TURN_U, 0)
                if c == SUM_AT:
                    pe.wait_ge(sum_split_ready, 2)
                    pe.wait_ge(lookup_out, LOOKUPS)
                    for q in range(QUADS):
                        ins = pe.matmul(bank[6][:, 0:LOOKUPS * CHUNKS * GROUPS],
                                        sum_split[:, (QUADS - 1 - q) * K:(2 * QUADS - 1 - q) * K],
                                        rows_split[:, :, q, :], start=(q == 0), stop=(q == QUADS - 1))
                    ins.then_inc(summed, 1)
                if c >= CROSS_BANKS:
                    pe.wait_ge(cross_out, c - CROSS_BANKS + 1)
                ps = bank[(c + CROSS_FIRST) % CROSS_BANKS]
                pe.matmul(ps[:, 0:NY], w2[:, c, :], wq_y[:, :], start=True, stop=True)
                pe.matmul(ps[:, NY:RCOLS], w2[:, c, :], wq_cross[:, part_of[c], :], start=True, stop=True).then_inc(cross_mm, 1)
            pe.wait_ge(cross_out, FIELDS - 2)
            t_matmuls(0, True)
            pe.wait_ge(cross_added, 1)
            turn(TURN_V, len(TURN_U))
            pe.wait_ge(mlp_loaded, MLP_LOADS)
            z_matmuls(0, True)
            dense_matmuls(0, range(2))
            with pe.Fori(1, CHUNKS) as c:
                mlp1(c - 1)
                pe.wait_ge(rows_in[D_EARLY], 16 * (ND - 1 - LATE) * (c + 1))
                mlp2(c - 1)
                t_matmuls(c, False)
                z_matmuls(c, False)
            mlp1(CHUNKS - 1)
            mlp2(CHUNKS - 1)
            mlp3(CHUNKS - 1)


def kernel(**inputs):
    import numpy as np
    import concourse.bacc as bacc
    from concourse.bass_utils import run_bass_kernel_spmd

    nc = bacc.Bacc("TRN2", target_bir_lowering=False, num_devices=1)
    laid_out = {
        "dense_t": np.ascontiguousarray(np.transpose(inputs["dense_ctx"])),
        "ids_rows": np.ascontiguousarray(np.reshape(np.transpose(inputs["ids"][:, list(LOOKED_UP)]), (1, LOOKUPS * BATCH))),
        "first_rows": np.arange(0, VROWS * VTILES, VTILES, dtype=np.float32).reshape(VROWS, 1),
        "ids": np.ascontiguousarray(inputs["ids"]),
        "w_top1": np.ascontiguousarray(inputs["W_top1"]),
        "b_top1": np.ascontiguousarray(np.transpose(np.reshape(inputs["b_top1"], (4, 128)))),
        "w_top2": np.ascontiguousarray(inputs["W_top2"]),
        "b_top2": np.ascontiguousarray(np.transpose(np.reshape(inputs["b_top2"], (2, 128)))),
        "w_top3": np.ascontiguousarray(np.transpose(np.reshape(inputs["W_top3"], (2, 128)))),
        "w1": np.ascontiguousarray(inputs["L0_rec_W1"]),
        "b1": np.ascontiguousarray(np.reshape(inputs["L0_rec_b1"], (128, 1))),
        "w2t": np.ascontiguousarray(np.transpose(inputs["L0_rec_W2"], (1, 2, 0))),
        "b2": np.ascontiguousarray(np.reshape(inputs["L0_rec_b2"], (128, 1))),
    }
    for f in range(FIELDS):
        laid_out[f"tbl_{f}"] = np.ascontiguousarray(inputs[f"tbl_{f}"])
    dram = {name: nc.dram_tensor(name, a.shape, mybir.dt.from_np(a.dtype), kind="ExternalInput").ap()
            for name, a in laid_out.items()}
    out = nc.dram_tensor("scores", (1, BATCH), mybir.dt.float32, kind="ExternalOutput").ap()
    tower_kernel(nc, dram["dense_t"], dram["ids"], dram["ids_rows"], dram["first_rows"],
                 [dram[f"tbl_{f}"] for f in range(FIELDS)],
                 dram["w_top1"], dram["b_top1"], dram["w_top2"], dram["b_top2"], dram["w_top3"],
                 dram["w1"], dram["b1"], dram["w2t"], dram["b2"], out)
    result = run_bass_kernel_spmd(nc, [laid_out], core_ids=[0])
    return np.reshape(result.results[0]["scores"], (BATCH, 1))
```
